# Optimizing a Trainium2 kernel written in Bass

```python
import numpy as np
import jax
import jax.numpy as jnp

def _softmax(x, axis=-1):
    return jax.nn.softmax(x, axis=axis)

def _gelu(x):
    return jax.nn.gelu(x, approximate=True)

def _silu(x):
    return jax.nn.silu(x)

def _sigmoid(x):
    return jax.nn.sigmoid(x)

def _layernorm(x, axis=-1, eps=1e-05):
    m = jnp.mean(x, axis=axis, keepdims=True)
    v = jnp.var(x, axis=axis, keepdims=True)
    return (x - m) / jnp.sqrt(v + eps)

def _scatter_add(tgt, idx, src, axis=0):
    return tgt.at[idx].add(src)

def _segment_sum(src, seg, n):
    return jax.ops.segment_sum(src, seg, n)
kernel_name = 'mk_decoder_preln_d1_seqx_r2_1687d3'

def setup_inputs(seed: int=0):
    np.random.seed(seed)
    _w = jnp.asarray

    def _rec_inputs():
        import jax
        import jax.numpy as jnp
        _rk = jax.random.key(seed)
        x = 7.22e-05 + 1 * jax.random.normal(jax.random.fold_in(_rk, 1), (16, 100, 512), jnp.float32)
        _lenS = 100 - jax.random.randint(jax.random.fold_in(_rk, 7), (16,), 0, max(1, 100 // 4) + 1, jnp.int32)
        _lenS2 = 722 - jax.random.randint(jax.random.fold_in(_rk, 8), (16,), 0, max(1, 722 // 4) + 1, jnp.int32)
        _ctx_768P = jax.random.normal(jax.random.fold_in(_rk, 11), (16, 16, 384), jnp.float32)
        _ctx_768c = jax.random.dirichlet(jax.random.fold_in(_rk, 511), 0.3 * jnp.ones((16,), jnp.float32), (16, 722))
        _ctx_768t = jnp.einsum('bsk,bkd->bsd', _ctx_768c, _ctx_768P)
        _ctx_768t = _ctx_768t * jax.lax.rsqrt(jnp.mean(jnp.square(_ctx_768t)) + 1e-12) * 0.953939
        ctx_768 = 2.09791e-05 + 1.00001 * (_ctx_768t + 0.3 * jax.random.normal(jax.random.fold_in(_rk, 611), (16, 722, 384), jnp.float32))
        return (x, ctx_768)
    x, ctx_768 = _rec_inputs()

    def _L0_attn_setup():
        import jax, jax.numpy as jnp
        import numpy as np
        N_HEAD = 16
        ROPE_BASE = 10000.0

        def _rope(Y, d_param):
            b, h, t, dh = Y.shape
            mid = d_param // 2
            Y1 = Y[:, :mid]
            Y2 = Y[:, mid:]
            Ym1 = jnp.concatenate([Y1, Y2], axis=1)
            Ym2 = jnp.concatenate([-Y2, Y1], axis=1)
            j = jnp.arange(t, dtype=Y.dtype)[:, None]
            i = jnp.arange(dh // 2, dtype=Y.dtype)[None, :]
            theta = j * jnp.power(jnp.asarray(ROPE_BASE, Y.dtype), -2.0 * i / dh)
            cos = jnp.cos(theta)
            sin = jnp.sin(theta)
            theta1 = jnp.concatenate([cos, cos], axis=1)
            theta2 = jnp.concatenate([sin, sin], axis=1)
            return Ym1 * theta1 + Ym2 * theta2
        key = jax.random.key(seed)
        ks = jax.random.split(key, 9)
        b, t, e = (2, 1024, 512)
        s = 1.0 / np.sqrt(e)
        return {'x': jax.random.normal(ks[0], (b, t, e), dtype=jnp.float32), 'Wq': jax.random.normal(ks[1], (e, e), dtype=jnp.float32) * s, 'bq': jax.random.normal(ks[2], (e,), dtype=jnp.float32) * 0.01, 'Wk': jax.random.normal(ks[3], (e, e), dtype=jnp.float32) * s, 'bk': jax.random.normal(ks[4], (e,), dtype=jnp.float32) * 0.01, 'Wv': jax.random.normal(ks[5], (e, e), dtype=jnp.float32) * s, 'bv': jax.random.normal(ks[6], (e,), dtype=jnp.float32) * 0.01, 'Wo': jax.random.normal(ks[7], (e, e), dtype=jnp.float32) * s, 'bo': jax.random.normal(ks[8], (e,), dtype=jnp.float32) * 0.01}
    _L0_attn_all = _L0_attn_setup()
    _L0_attn_in = {k: v for k, v in _L0_attn_all.items() if k in ('Wq', 'bq', 'Wk', 'bk', 'Wv', 'bv', 'Wo', 'bo')}
    del _L0_attn_all

    def _L0_xattn_setup():
        import jax, jax.numpy as jnp
        import numpy as np
        NUM_HEADS = 16
        key = jax.random.key(seed)
        ks = jax.random.split(key, 8)
        dim, cond_dim = (512, 384)
        B, N, condN = (4, 1024, 512)
        s = lambda k, shp, fan: jax.random.normal(k, shp, dtype=jnp.float32) * fan ** (-0.5)
        return {'x': jax.random.normal(ks[0], (B, N, dim), dtype=jnp.float32), 'cond': jax.random.normal(ks[1], (B, condN, cond_dim), dtype=jnp.float32), 'q_w': s(ks[2], (dim, dim), dim), 'q_b': jnp.zeros((dim,), jnp.float32), 'kv_w': s(ks[3], (cond_dim, 2 * dim), cond_dim), 'kv_b': jnp.zeros((2 * dim,), jnp.float32), 'proj_w': s(ks[4], (dim, dim), dim), 'proj_b': jnp.zeros((dim,), jnp.float32)}
    _L0_xattn_all = _L0_xattn_setup()
    _L0_xattn_in = {k: v for k, v in _L0_xattn_all.items() if k in ('q_w', 'q_b', 'kv_w', 'kv_b', 'proj_w', 'proj_b')}
    del _L0_xattn_all

    def _L0_ffn_setup():
        import jax, jax.numpy as jnp
        import numpy as np
        TOP_K = 2
        key = jax.random.key(seed)
        k1, k2, k3 = jax.random.split(key, 3)
        B, S, H, E = (4, 1024, 512, 8)
        x = jax.random.normal(k1, (B, S, H), dtype=jnp.float32)
        gate_w = jax.random.normal(k2, (E, H), dtype=jnp.float32) / np.sqrt(H)
        gate_b = jnp.zeros((E,), dtype=jnp.float32)
        expert_w = jax.random.normal(k3, (E, H, H), dtype=jnp.float32) / np.sqrt(H)
        expert_b = jnp.zeros((E, H), dtype=jnp.float32)
        return {'x': x, 'gate_w': gate_w, 'gate_b': gate_b, 'expert_w': expert_w, 'expert_b': expert_b}
    _L0_ffn_all = _L0_ffn_setup()
    _L0_ffn_in = {k: v for k, v in _L0_ffn_all.items() if k in ('gate_w', 'gate_b', 'expert_w', 'expert_b')}
    del _L0_ffn_all
    return {'x': x, 'ctx_768': ctx_768, 'L0_attn_Wq': _L0_attn_in['Wq'], 'L0_attn_bq': _L0_attn_in['bq'], 'L0_attn_Wk': _L0_attn_in['Wk'], 'L0_attn_bk': _L0_attn_in['bk'], 'L0_attn_Wv': _L0_attn_in['Wv'], 'L0_attn_bv': _L0_attn_in['bv'], 'L0_attn_Wo': _L0_attn_in['Wo'], 'L0_attn_bo': _L0_attn_in['bo'], 'L0_xattn_q_w': _L0_xattn_in['q_w'], 'L0_xattn_q_b': _L0_xattn_in['q_b'], 'L0_xattn_kv_w': _L0_xattn_in['kv_w'], 'L0_xattn_kv_b': _L0_xattn_in['kv_b'], 'L0_xattn_proj_w': _L0_xattn_in['proj_w'], 'L0_xattn_proj_b': _L0_xattn_in['proj_b'], 'L0_ffn_gate_w': _L0_ffn_in['gate_w'], 'L0_ffn_gate_b': _L0_ffn_in['gate_b'], 'L0_ffn_expert_w': _L0_ffn_in['expert_w'], 'L0_ffn_expert_b': _L0_ffn_in['expert_b']}

def reference(x, ctx_768, L0_attn_Wq, L0_attn_bq, L0_attn_Wk, L0_attn_bk, L0_attn_Wv, L0_attn_bv, L0_attn_Wo, L0_attn_bo, L0_xattn_q_w, L0_xattn_q_b, L0_xattn_kv_w, L0_xattn_kv_b, L0_xattn_proj_w, L0_xattn_proj_b, L0_ffn_gate_w, L0_ffn_gate_b, L0_ffn_expert_w, L0_ffn_expert_b):
    import jax
    import jax.numpy as jnp

    def _L0_attn_ref(x, Wq, bq, Wk, bk, Wv, bv, Wo, bo):
        import jax, jax.numpy as jnp
        import numpy as np
        N_HEAD = 16
        ROPE_BASE = 10000.0

        def _rope(Y, d_param):
            b, h, t, dh = Y.shape
            mid = d_param // 2
            Y1 = Y[:, :mid]
            Y2 = Y[:, mid:]
            Ym1 = jnp.concatenate([Y1, Y2], axis=1)
            Ym2 = jnp.concatenate([-Y2, Y1], axis=1)
            j = jnp.arange(t, dtype=Y.dtype)[:, None]
            i = jnp.arange(dh // 2, dtype=Y.dtype)[None, :]
            theta = j * jnp.power(jnp.asarray(ROPE_BASE, Y.dtype), -2.0 * i / dh)
            cos = jnp.cos(theta)
            sin = jnp.sin(theta)
            theta1 = jnp.concatenate([cos, cos], axis=1)
            theta2 = jnp.concatenate([sin, sin], axis=1)
            return Ym1 * theta1 + Ym2 * theta2
        b, t, e = x.shape
        h = N_HEAD
        dh = e // h

        def proj(W, bias):
            y = jnp.einsum('bte,fe->btf', x, W) + bias
            return y.reshape(b, t, h, dh).transpose(0, 2, 1, 3)
        q = _rope(proj(Wq, bq), e)
        k = _rope(proj(Wk, bk), e)
        v = proj(Wv, bv)
        scale = jnp.sqrt(jnp.asarray(dh, x.dtype))
        att = jnp.einsum('bhqd,bhkd->bhqk', q, k) / scale
        causal = jnp.tril(jnp.ones((t, t), dtype=bool))
        att = jnp.where(causal[None, None], att, -jnp.inf)
        att = jax.nn.softmax(att, axis=-1)
        y = jnp.einsum('bhqk,bhkd->bhqd', att, v)
        y = y.transpose(0, 2, 1, 3).reshape(b, t, e)
        return jnp.einsum('bte,fe->btf', y, Wo) + bo

    def _L0_xattn_ref(x, cond, q_w, q_b, kv_w, kv_b, proj_w, proj_b):
        import jax, jax.numpy as jnp
        import numpy as np
        NUM_HEADS = 16
        B, N, C = x.shape
        condN = cond.shape[1]
        H = NUM_HEADS
        hd = C // H
        scale = hd ** (-0.5)
        q = (x @ q_w + q_b).reshape(B, N, H, hd).transpose(0, 2, 1, 3)
        kv = (cond @ kv_w + kv_b).reshape(B, condN, 2, H, hd)
        k = kv[:, :, 0].transpose(0, 2, 1, 3)
        v = kv[:, :, 1].transpose(0, 2, 1, 3)
        attn = jnp.einsum('bhnd,bhmd->bhnm', q * scale, k)
        attn = jax.nn.softmax(attn, axis=-1)
        out = jnp.einsum('bhnm,bhmd->bhnd', attn, v)
        out = out.transpose(0, 2, 1, 3).reshape(B, N, C)
        return out @ proj_w + proj_b

    def _L0_ffn_ref(x, gate_w, gate_b, expert_w, expert_b):
        import jax, jax.numpy as jnp
        import numpy as np
        TOP_K = 2
        gates = jax.nn.softmax(jnp.einsum('bsh,eh->bse', x, gate_w) + gate_b, axis=-1)
        top_gates, top_idx = jax.lax.top_k(gates, TOP_K)
        expert_out = jnp.einsum('bsh,eoh->bseo', x, expert_w) + expert_b
        selected = jnp.take_along_axis(expert_out, top_idx[..., None], axis=2)
        return (selected * top_gates[..., None]).sum(axis=2)
    x = x + _L0_attn_ref(_layernorm(x, axis=-1), L0_attn_Wq, L0_attn_bq, L0_attn_Wk, L0_attn_bk, L0_attn_Wv, L0_attn_bv, L0_attn_Wo, L0_attn_bo)
    x = x + _L0_xattn_ref(_layernorm(x, axis=-1), ctx_768, L0_xattn_q_w, L0_xattn_q_b, L0_xattn_kv_w, L0_xattn_kv_b, L0_xattn_proj_w, L0_xattn_proj_b)
    x = x + _L0_ffn_ref(_layernorm(x, axis=-1), L0_ffn_gate_w, L0_ffn_gate_b, L0_ffn_expert_w, L0_ffn_expert_b)
    return x

_drawn_inputs = setup_inputs


def setup_inputs(seed=0):
    import zlib

    import numpy as np

    out = dict(_drawn_inputs(seed))
    spreads = {'L0_xattn_q_b': (0.0, 0.1),
     'L0_xattn_kv_b': (0.0, 0.1),
     'L0_xattn_proj_b': (0.0, 0.1),
     'L0_ffn_gate_b': (0.0, 0.1),
     'L0_ffn_expert_b': (0.0, 0.1)}
    factors = {'L0_attn_bq': 5.293, 'L0_attn_bk': 7.768, 'L0_attn_bv': 2.767, 'L0_attn_bo': 4.028}
    for name, (base, spread) in spreads.items():
        noise = np.random.default_rng([zlib.crc32(name.encode()), seed]).standard_normal(out[name].shape)
        drawn = base * np.exp(spread * noise) if base else spread * noise
        out[name] = jnp.asarray(drawn.astype(out[name].dtype))
    for name, factor in factors.items():
        out[name] = (out[name] * factor).astype(out[name].dtype)
    return out
```

```python
from contextlib import ExitStack

import concourse.bass as bass
import numpy as np
from concourse import mybir

F32 = mybir.dt.float32
F16 = mybir.dt.float16
ALU = mybir.AluOpType
ACT = mybir.ActivationFunctionType
AXIS = mybir.AxisListType

P = 128
B, L, D = 16, 100, 512
LC, DC = 722, 384
H, DH = 16, 32
E = 8
T = B * L
KD, KC = D // P, DC // P
HT = P // DH
CT = 6
CW = 121
LCP = CT * CW
HC = LC // 2
HP = LCP // 2
TT = (T + P - 1) // P
TLAST = T - (TT - 1) * P
WSCALE = 32.0
PSCALE = 1.0 / (WSCALE * WSCALE)
SOFT = PSCALE / float(np.sqrt(DH))
EPS = 1e-5
MASKED = -1e30
BANK = 512
OCOL = 304
KLOW, KHIGH, QLOW, QHIGH = range(4)

STEP_CHUNKS = [
    ["X1T", "CX0"],
    ["SQ", "SK", "CX1"],
    ["SV", "CX2", "CX3"],
    ["TT", "CX4", "CX5"],
    ["SS0", "SS1", "TP"],
    ["SS2", "SS3", "CK0"],
    ["CK1", "CK2"],
    ["SP0", "SP1", "CK3"],
    ["SP2", "SP3", "CK4"],
    ["SO", "CK5", "CK6"],
    ["OT", "CK7"],
    ["OP", "CV0", "CV1"],
    ["CV2", "X2T", "CV3"],
    ["CQ", "CV4"],
    ["CV5"],
    [],
]
SPLIT = ("X1T", "SV", "SP0", "SP1", "SP2", "SP3", "OT", "X2T", "TT") + tuple(
    [f"CX{c}" for c in range(6)] + [f"CK{c}" for c in range(8)] + [f"CV{c}" for c in range(6)])


class Iteration:

    def __init__(self, n, odd, cross=True, prep=True, tail=True):
        self.n, self.odd, self.cross, self.prep, self.tail = n, odd, cross, prep, tail
        self.steps = [[c for c in step if (tail if c in ("TT", "TP") else prep)] for step in STEP_CHUNKS]
        self.order = [c for step in self.steps for c in step]

    @staticmethod
    def _count(names):
        return len(names), sum(c in SPLIT for c in names)

    def _before(self, which):
        every = [c for step in STEP_CHUNKS for c in step]
        head = self._count([c for c in every if c not in ("TT", "TP")])[which]
        each = self._count(every)[which]
        if isinstance(self.n, int):
            return 0 if self.n < 0 else head if self.n == 0 else (
                2 * head + (min(self.n, B - 1) - 1) * each + (self.n - B + 1 > 0) * self._count(["TT", "TP"])[which])
        return 2 * head + (self.n - 1) * each

    def bank(self, chunk):
        every = sum(len(s) for s in STEP_CHUNKS)
        head = every - 2
        if isinstance(self.n, int):
            start = self._before(0)
        else:
            start = 2 * head + (0 if self.odd else every)
        return (start + self.order.index(chunk)) % 2

    def done(self, chunk):
        return self._before(0) + self.order.index(chunk) + 1

    def high_done(self, chunk):
        return self._before(1) + sum(c in SPLIT for c in self.order[:self.order.index(chunk) + 1])

    def all_before(self):
        return self._before(0)


def build_layer(nc, x, ctx, sWq, sbq, sWk, sbk, sWv, sbv, sWo, sbo, cWq, cbq, cWkv, cbkv, cWp, cbp,
                gW, gb, eW, eb, rope, x2_dram, out):
    with ExitStack() as stack:
        def sb(name, shape, dt=F32):
            return stack.enter_context(nc.sbuf_tensor(name, shape, dt))

        def sem(name):
            return stack.enter_context(nc.semaphore(name))

        w_self_all = sb("w_self_all", [P, 4, KD, 2, D], F16)
        w_self = {k: w_self_all[:, i] for i, k in enumerate("qkvo")}
        w_cross = {k: sb(f"w_cross_{k}", [P, KD, 2, D], F16) for k in "qp"}
        w_kv = sb("w_kv", [P, KC, 2, 2 * D], F16)
        ident = sb("ident", [P, P])
        mask = sb("mask", [L, L])
        rope_t = sb("rope_t", [P, L])
        b_part = sb("b_part", [P, 6, KD])
        b_rows = sb("b_rows", [6 * KD, P])
        b_value = sb("b_value", [P, 2, 2, KD], F16)
        b_so, b_cp = sb("b_so", [L, D]), sb("b_cp", [L, D])
        half = sb("half", [P, 1])
        x_in = sb("x_in", [L, D])
        x_norm = sb("x_norm", [L, D])
        s_out = x_norm
        x_mid = [sb(f"x_mid{i}", [L, D]) for i in range(2)]
        xT = sb("xT", [P, 2, KD, L], F16)
        stats = sb("stats", [P, 6])
        moments = sb("moments", [P, 2])
        shift = sb("shift", [P, 2])
        rstd = sb("rstd", [P, 1])
        tmp_q, tmp_k = sb("tmp_q", [P, KD, L]), sb("tmp_k", [P, KD, L])
        split_qk = sb("split_qk", [P, 4, KD, L], F16)
        stack_qk = sb("stack_qk", [3 * DH, 2, H, L], F16)
        stack_q = [sb(f"stack_q{i}", [3 * DH, H, L], F16) for i in range(2)]
        sv = sb("sv", [L, 2, D], F16)
        c_raw = sb("c_raw", [CW, CT, DC])
        c_flat = c_raw[:].rearrange("p t c -> p (t c)")
        s_sc = c_flat[0:L, 0:H * L].rearrange("q (g c) -> q g c", g=4)
        s_scT = s_sc.bitcast(F16)
        s_max, s_sum, s_rinv = sb("s_max", [L, H]), sb("s_sum", [L, H]), sb("s_rinv", [L, H])
        oT = xT
        cT = sb("cT", [P, KC, 2, LCP], F16)
        split_k = sb("split_k", [P, 2, KD, LC], F16)
        cv = [sb(f"cv{i}", [CW, 2, CT, D], F16) for i in range(2)]
        prob = [sb(f"prob{i}", [L, LCP]) for i in range(2)]
        probT = sb("probT", [CW, 2, CT * L], F16)
        c_max, c_bias, c_sum, c_rinv = (sb(n, [L, 2, H]) for n in ("c_max", "c_bias", "c_sum", "c_rinv"))
        c_out = sb("c_out", [L, D])
        arena = sb("arena", [P, 2, H, LC], F16)
        stack_k = [arena[0:3 * DH, i] for i in range(2)]
        flat32 = arena[:].rearrange("p a h c -> p (a h c)").bitcast(F32)

        psum = stack.enter_context(nc.psum_tensor("psum", [P, 8, BANK], F32))
        score = [psum[:, 2 * i:2 * i + 2] for i in range(2)]
        pT = psum[:, 4:6]
        filler = [psum[:, 6], psum[:, 7]]

        const_loaded, setup_done, ident_done = sem("const_loaded"), sem("setup_done"), sem("ident_done")
        bias_ready_T, bias_done = sem("bias_ready_T"), sem("bias_done")
        raw_loaded = [sem(f"raw_loaded{i}") for i in range(5)]
        raw2_loaded = sem("raw2_loaded")
        wT_ready, wT_high, wT_low = sem("wT_ready"), sem("wT_high"), sem("wT_low")
        w_high, w_low = sem("w_high"), sem("w_low")
        x_loaded, ctx_loaded = sem("x_loaded"), sem("ctx_loaded")
        chunk_ready, chunk_high, chunk_out = sem("chunk_ready"), sem("chunk_high"), sem("chunk_out")
        bn_done, stats_done, ln_shift, ln_rstd, norm_done = (
            sem(n) for n in ("bn_done", "stats_done", "ln_shift", "ln_rstd", "norm_done"))
        x_biased = sem("x_biased")
        qk_rotated, qk_high, qk_split, qk_stacked = (
            sem(n) for n in ("qk_rotated", "qk_high", "qk_split", "qk_stacked"))
        cq_high, cq_split, cq_stacked = sem("cq_high"), sem("cq_split"), sem("cq_stacked")
        s_max_done, s_shifted, s_exp, s_sum_done, s_rinv_done = (
            sem(n) for n in ("s_max_done", "s_shifted", "s_exp", "s_sum_done", "s_rinv_done"))
        k_stacked = sem("k_stacked")
        score_ready, max_done, bias_ready, exp_done = (
            sem(n) for n in ("score_ready", "max_done", "bias_ready", "exp_done"))
        pT_ready, pT_high, pT_low, pT_out, head_done = (
            sem(n) for n in ("pT_ready", "pT_high", "pT_low", "pT_out", "head_done"))
        c_rinv_done, c_out_done = sem("c_rinv_done"), sem("c_out_done")
        bv_high, bv_split, bv_ready, bv_folded = (sem(n) for n in ("bv_high", "bv_split", "bv_ready", "bv_folded"))
        x2_stored = sem("x2_stored")

        wait_over = sem("wait_over")

        def wait_alone(engine, semaphore, value):
            engine.wait_ge(semaphore, value)
            if not isinstance(value, int):
                engine.sem_inc(wait_over, 1)

        def split3(pe, out_ap, pairs):
            last = None
            for i, (a, b) in enumerate(pairs):
                for j, (pa, pb) in enumerate(((0, 0), (0, 1), (1, 0))):
                    last = pe.matmul(out_ap, a(pa), b(pb), start=(i == 0 and j == 0),
                                     stop=(i == len(pairs) - 1 and j == 2))
            return last

        xT3 = arena[:].rearrange("p a h c -> p (a h c)")[:, 0:2 * KD * TT * P]\
            .rearrange("p (s k t) -> p s k t", s=2, k=KD)
        raw_e = [flat32[:, KD * TT * P + i * KD * D:KD * TT * P + (i + 1) * KD * D]
                 .rearrange("p (o h) -> p o h", o=KD) for i in range(2)]
        self32 = w_self_all[:].rearrange("p w k s f -> p (w k s f)").bitcast(F32)
        y = self32[:, 0:TT * D].rearrange("p (t d) -> p t d", t=TT)
        y_norm = [self32[:, (TT + i) * D:(TT + i + 1) * D] for i in range(2)]
        wT_e = [w_cross["q"], w_cross["p"]]
        stats3, moments3 = sb("stats3", [P, 2, 6]), sb("moments3", [P, TT, 2])
        rstd3, nmean3 = sb("rstd3", [P, TT]), sb("nmean3", [P, TT])
        g_raw, g_T, g_bias = x_in[0:E], sb("g_T", [P, 2, KD, E], F16), sb("g_bias", [P, E])
        k_flat = split_k[:].rearrange("p s k c -> p (s k c)").bitcast(F32)
        gates, picked, first, tie, g_scaled = (
            k_flat[:, i * TT * E:(i + 1) * TT * E].rearrange("p (t e) -> p t e", e=E) for i in range(5))
        rank = sb("rank", [P, E])
        best = sb("best", [P, TT])
        g_now = sb("g_now", [P, 2, TT])
        gT_tok = c_flat[0:E, 0:TT * P].rearrange("e (t p) -> e t p", t=TT)
        e_bias = c_flat[0:E, TT * P:TT * P + D]

        y_zeroed, g_loaded = sem("y_zeroed"), sem("g_loaded")
        y_loaded = [sem(f"y_loaded{t}") for t in range(TT)]
        e_loaded = [sem(f"e_loaded{i}") for i in range(2)]
        f_bn, f_stats, f_half, f_rstd, f_norm = (sem(n) for n in ("f_bn", "f_stats", "f_half", "f_rstd", "f_norm"))
        f_T, f_high, f_low = sem("f_T"), sem("f_high"), sem("f_low")
        gT_ready, gT_high, gT_low = sem("gT_ready"), sem("gT_high"), sem("gT_low")
        logits_ready, route, g_exp = sem("logits_ready"), sem("route"), sem("g_exp")
        tokT_ready, tokT_out, eb_ready, eb_out = (sem(n) for n in ("tokT_ready", "tokT_out", "eb_ready", "eb_out"))
        e_T, e_high, e_low = sem("e_T"), sem("e_high"), sem("e_low")
        g_now_set, y_ready, y_done, y_stored = (sem(n) for n in ("g_now_set", "y_ready", "y_done", "y_stored"))
        rank_set = sem("rank_set")

        last_it = Iteration(B, False, cross=False, prep=False)
        ALL_CHUNKS = last_it.all_before() + 2
        ROUTED = 21

        def experts(engine, body):
            body(0, 0, 0, True)
            with engine.Fori(0, (E - 4) // 2) as i:
                body(2 * i + 1, 1, i, True)
                body(2 * i + 2, 0, i + 1, True)
            for e in range(E - 3, E):
                body(e, e % 2, e // 2, e < E - 1)

        def load_expert(sp, e, odd):
            sp.dma_start(raw_e[odd], eW[e].rearrange("(o p) h -> p o h", p=P)).then_inc(e_loaded[odd], 16)

        def ffn_sync(sp):
            sp.wait_ge(chunk_out, ALL_CHUNKS)
            sp.wait_ge(x2_stored, 16 * B)
            sp.wait_ge(y_zeroed, 1)
            sp.dma_start(g_raw, gW).then_inc(g_loaded, 16)
            sp.dma_start(e_bias, eb).then_inc(g_loaded, 16)
            for t in range(TT):
                n = min(P, T - t * P)
                sp.dma_start(y[0:n, t], x2_dram.rearrange("b l d -> (b l) d")[t * P:t * P + n]).then_inc(y_loaded[t], 16)
                if t == 3:
                    load_expert(sp, 0, 0)
            load_expert(sp, 1, 1)

            def next_raw(e, odd, pair, more):
                if not isinstance(e, int) or e < E - 2:
                    wait_alone(sp, e_low, KD * (e + 1))
                    load_expert(sp, e + 2, odd)
            experts(sp, next_raw)
            for t in range(TT):
                n = min(P, T - t * P)
                sp.wait_ge(y_done, TT * (E - 1) + t + 1)
                sp.dma_start(out.rearrange("b l d -> (b l) d")[t * P:t * P + n], y[0:n, t]).then_inc(y_stored, 16)
            sp.wait_ge(y_stored, 16 * TT)

        def pe_expert_T(pe, e, odd, pair, k):
            c = KD * e + k
            if k == 0:
                pe.wait_ge(e_loaded[odd], 16 * (pair + 1))
            if not (isinstance(c, int) and c < 2):
                pe.wait_ge(e_low, c - 1)
            for o in range(KD):
                last = pe.transpose(psum[:, 4 + k % 2, o * P:(o + 1) * P], raw_e[odd][:, o, k * P:(k + 1) * P], ident[:])
            last.then_inc(e_T, 1)

        def ffn_tensor(pe):
            pe.wait_ge(chunk_out, ALL_CHUNKS)
            pe.wait_ge(g_loaded, 32)
            for k in range(KD):
                last = pe.transpose(psum[:, 7, k * E:(k + 1) * E], g_raw[:, k * P:(k + 1) * P], ident[0:E, 0:E])
            last.then_inc(gT_ready, 1)
            pe.wait_ge(gT_low, 1)
            for t in range(TT):
                pe.wait_ge(f_norm, t + 1)
                if t >= 4:
                    pe.wait_ge(f_low, t - 3)
                for k in range(KD):
                    last = pe.transpose(psum[:, t % 4, k * P:(k + 1) * P], y_norm[t % 2][:, k * P:(k + 1) * P], ident[:])
                last.then_inc(f_T, 1)
                if t >= 1:
                    pe_logits(pe, t - 1)
            pe_logits(pe, TT - 1).then_inc(logits_ready, 1)
            for k in range(KD):
                pe_expert_T(pe, 0, 0, 0, k)
            pe.wait_ge(route, ROUTED)
            for t in range(TT):
                if t >= 4 and t % 4 == 0:
                    pe.wait_ge(tokT_out, t // 4)
                last = pe.transpose(psum[0:E, 6, (t % 4) * P:(t % 4 + 1) * P], gates[:, t], ident[:])
                if t % 4 == 3 or t == TT - 1:
                    last.then_inc(tokT_ready, 1)
            for t in range(TT):
                pe.wait_ge(tokT_out, t // 4 + 1)
                if t >= 2:
                    pe.wait_ge(eb_out, t - 1)
                pe.matmul(psum[:, 2 + t % 2, 0:D], gT_tok[:, t], e_bias, start=True, stop=True).then_inc(eb_ready, 1)

            def expert(e, odd, pair, more):
                for t in range(TT):
                    c = TT * e + t
                    if t == 0:
                        pe.wait_ge(e_low, KD * (e + 1))
                    if not (isinstance(e, int) and c < 2):
                        pe.wait_ge(y_done, c - 1)
                    split3(pe, psum[:, (t + odd) % 4, 0:D],
                           [(lambda p, k=k: xT3[:, p, k, t * P:(t + 1) * P], lambda p, k=k: wT_e[odd][:, k, p])
                            for k in range(KD)]).then_inc(y_ready, 1)
                    if more and t % 3 == 1 and t // 3 < KD:
                        pe_expert_T(pe, e + 1, 1 - odd, pair + odd, t // 3)
            pe.wait_ge(eb_out, TT)
            experts(pe, expert)

        def pe_logits(pe, t):
            pe.wait_ge(f_low, t + 1)
            return split3(pe, psum[:, 7, 64 + t * E:64 + (t + 1) * E],
                          [(lambda p, k=k: xT3[:, p, k, t * P:(t + 1) * P], lambda p, k=k: g_T[:, p, k])
                           for k in range(KD)])

        def ffn_scalar(act):
            act.wait_ge(gT_ready, 1)
            act.activation(g_T[:, 0].rearrange("p k e -> p (k e)"), psum[:, 7, 0:KD * E], ACT.Copy, scale=WSCALE)\
               .then_inc(gT_high, 1)
            for t in range(TT):
                act.wait_ge(f_T, t + 1)
                act.activation(xT3[:, 0, :, t * P:(t + 1) * P], psum[:, t % 4].rearrange("p (k t) -> p k t", k=KD),
                               ACT.Copy).then_inc(f_high, 1)

            def expert_high(e, odd, k):
                act.wait_ge(e_T, KD * e + k + 1)
                act.activation(wT_e[odd][:, k, 0], psum[:, 4 + k % 2], ACT.Copy, scale=WSCALE).then_inc(e_high, 1)
            for k in range(KD):
                expert_high(0, 0, k)
            act.wait_ge(route, 3)
            act.activation(gates, gates, ACT.Exp).then_inc(g_exp, 1)
            for i in range((TT + 3) // 4):
                act.wait_ge(tokT_ready, i + 1)
                n = min(4, TT - 4 * i)
                act.activation(gT_tok[:, 4 * i:4 * i + n].rearrange("e t p -> e (t p)"), psum[0:E, 6, 0:n * P],
                               ACT.Copy).then_inc(tokT_out, 1)
            experts(act, lambda e, odd, pair, more: [expert_high(e + 1, 1 - odd, k) for k in range(KD)] if more else None)

        def ffn_vector(dve):
            dve.wait_ge(chunk_out, ALL_CHUNKS)
            dve.memset(y[TLAST:P, TT - 1], 0.0).then_inc(y_zeroed, 1)
            dve.wait_ge(gT_high, 1)
            dve.scalar_tensor_tensor(g_T[:, 1].rearrange("p k e -> p (k e)"), psum[:, 7, 0:KD * E], WSCALE,
                                     g_T[:, 0].rearrange("p k e -> p (k e)"), ALU.mult, ALU.subtract)\
               .then_inc(gT_low, 1)
            for t in range(TT):
                dve.wait_ge(y_loaded[t], 16)
                if t >= 2:
                    dve.wait_ge(f_stats, t - 1)
                dve.bn_stats(stats3[:, t % 2], y[:, t]).then_inc(f_bn, 1)
                dve.wait_ge(f_bn, t + 1)
                dve.bn_aggr(moments3[:, t], stats3[:, t % 2]).then_inc(f_stats, 1)

            def low(t):
                dve.wait_ge(f_high, t + 1)
                dve.tensor_tensor(xT3[:, 1, :, t * P:(t + 1) * P], psum[:, t % 4].rearrange("p (k t) -> p k t", k=KD),
                                  xT3[:, 0, :, t * P:(t + 1) * P], ALU.subtract).then_inc(f_low, 1)
            dve.wait_ge(f_rstd, 1)
            for t in range(TT):
                if t >= 2:
                    dve.wait_ge(f_T, t - 1)
                dve.tensor_scalar(y_norm[t % 2], y[:, t], nmean3[:, t:t + 1], rstd3[:, t:t + 1], ALU.add, ALU.mult)\
                   .then_inc(f_norm, 1)
                if t >= 1:
                    low(t - 1)
            low(TT - 1)

            def expert_low(e, odd, k):
                dve.wait_ge(e_high, KD * e + k + 1)
                dve.scalar_tensor_tensor(wT_e[odd][:, k, 1], psum[:, 4 + k % 2], WSCALE, wT_e[odd][:, k, 0],
                                         ALU.mult, ALU.subtract).then_inc(e_low, 1)
            done = [0]

            def step(op):
                op.then_inc(route, 1)
                done[0] += 1
                dve.wait_ge(route, done[0])

            def over(a):
                return a[:].unsqueeze(2).to_broadcast([P, TT, E])
            dve.wait_ge(logits_ready, 1)
            step(dve.scalar_tensor_tensor(gates, psum[:, 7, 64:64 + TT * E].rearrange("p (t e) -> p t e", e=E),
                                          1.0 / WSCALE, g_bias[:].unsqueeze(1).to_broadcast([P, TT, E]),
                                          ALU.mult, ALU.add))
            step(dve.tensor_reduce(best[:], gates, AXIS.X, ALU.max))
            step(dve.tensor_tensor(gates, gates, over(best), ALU.subtract))
            for k in range(KD):
                expert_low(0, 0, k)
            dve.wait_ge(g_exp, 1)
            step(dve.tensor_reduce(best[:], gates, AXIS.X, ALU.add))
            step(dve.reciprocal(best[:], best[:]))
            step(dve.tensor_tensor(gates, gates, over(best), ALU.mult))
            dve.wait_ge(rank_set, E)
            for i in range(2):
                src = gates if i == 0 else tie
                step(dve.tensor_reduce(best[:], src, AXIS.X, ALU.max))
                step(dve.tensor_tensor(first, src, over(best), ALU.is_ge))
                step(dve.tensor_tensor(first, first, rank[:].unsqueeze(1).to_broadcast([P, TT, E]), ALU.mult))
                step(dve.tensor_reduce(best[:], first, AXIS.X, ALU.max))
                if i == 0:
                    step(dve.tensor_tensor(picked, first, over(best), ALU.is_equal))
                    step(dve.scalar_tensor_tensor(tie, picked, -4.0, gates, ALU.mult, ALU.add))
                else:
                    step(dve.tensor_tensor(first, first, over(best), ALU.is_equal))
                    step(dve.tensor_tensor(picked, picked, first, ALU.add))
            step(dve.tensor_tensor(gates, gates, picked, ALU.mult))
            step(dve.tensor_scalar(g_scaled, gates, 1.0 / WSCALE, None, ALU.mult))
            step(dve.tensor_copy(g_now[:, 0], g_scaled[:, :, 0]))
            assert done[0] == ROUTED
            for t in range(TT):
                dve.wait_ge(eb_ready, t + 1)
                dve.tensor_tensor(y[:, t], psum[:, 2 + t % 2, 0:D], y[:, t], ALU.add).then_inc(eb_out, 1)

            def expert(e, odd, pair, more):
                dve.wait_ge(y_done, TT * e) if not isinstance(e, int) or e > 0 else None
                dve.tensor_copy(g_now[:, odd], g_scaled[:, :, e]).then_inc(g_now_set, 1)
                dve.wait_ge(g_now_set, e + 1)
                for t in range(TT):
                    dve.wait_ge(y_ready, TT * e + t + 1)
                    dve.scalar_tensor_tensor(y[:, t], psum[:, (t + odd) % 4, 0:D], g_now[:, odd, t:t + 1], y[:, t],
                                             ALU.mult, ALU.add).then_inc(y_done, 1)
                    if more and t % 3 == 1 and t // 3 < KD:
                        expert_low(e + 1, 1 - odd, t // 3)
            dve.wait_ge(eb_out, TT)
            experts(dve, expert)

        def ffn_gpsimd(pool):
            pool.wait_ge(f_stats, TT)
            pool.tensor_scalar(nmean3[:], moments3[:, :, 0], -1.0, None, ALU.mult).then_inc(f_half, 1)
            pool.tensor_scalar(rstd3[:], moments3[:, :, 1], EPS, None, ALU.add).then_inc(f_half, 1)
            pool.wait_ge(f_half, 2)
            pool.tensor_tensor(rstd3[:], rstd3[:], half[:].to_broadcast([P, TT]), ALU.pow).then_inc(f_rstd, 1)


        def pipeline(engine, body):
            peel_from = B - 3
            body(Iteration(-1, True, cross=False, tail=False))
            body(Iteration(0, False, tail=False))
            with engine.Fori(0, (peel_from - 1) // 2) as i:
                body(Iteration(2 * i + 1, True))
                body(Iteration(2 * i + 2, False))
            for n in range(peel_from, B):
                body(Iteration(n, n % 2 == 1, prep=n < B - 1))
            body(Iteration(B, False, cross=False, prep=False))

        block = stack.enter_context(nc.Block())

        def load_x(sp, m):
            sp.dma_start(x_in[:], x[m]).then_inc(x_loaded, 16)

        def load_ctx(sp, m):
            full = CT - 1
            sp.dma_start(c_raw[:, 0:full], ctx[m, 0:full * CW].rearrange("(t p) c -> p t c", p=CW))\
              .then_inc(ctx_loaded, 16)
            sp.dma_start(c_raw[0:LC - full * CW, full], ctx[m, full * CW:LC]).then_inc(ctx_loaded, 16)

        def sync_iteration(sp, it):
            n, m = it.n, it.n + 1
            if it.prep:
                wait_alone(sp, qk_split, 2 * m + 2)
                if not (isinstance(n, int) and n < 0):
                    wait_alone(sp, chunk_out, it.all_before())
                for j in range(HT):
                    for r, slots in enumerate(((KHIGH, QHIGH), (KHIGH, QLOW), (KLOW, QHIGH))):
                        for i, slot in enumerate(slots):
                            sp.dma_start(stack_qk[DH * r:DH * (r + 1), i, j::HT],
                                         split_qk[DH * j:DH * (j + 1), slot]).then_inc(qk_stacked, 16)
            if it.prep and not (isinstance(n, int) and n == B - 2):
                wait_alone(sp, chunk_out, it.done("SO"))
                load_ctx(sp, n + 2)
            if it.tail:
                wait_alone(sp, chunk_out, it.done("TP"))
                sp.dma_start(x2_dram[n - 1], x_mid[1 if not it.odd else 0][:]).then_inc(x2_stored, 16)
            if it.prep:
                odd_m = not it.odd
                if it.tail:
                    wait_alone(sp, score_ready, H * n)
                wait_alone(sp, chunk_out, it.done(f"CK{2 * KD - 1}"))
                for c in range(HT):
                    for r, part in enumerate((0, 0, 1)):
                        sp.dma_start(stack_k[odd_m][DH * r:DH * (r + 1), c::HT],
                                     split_k[DH * c:DH * (c + 1), part]).then_inc(k_stacked, 16)
                if not (isinstance(n, int) and n == B - 2):
                    wait_alone(sp, chunk_out, it.done("OP"))
                    load_x(sp, n + 2)
                wait_alone(sp, cq_split, m + 1)
                for c in range(HT):
                    for r, slot in enumerate((QHIGH, QLOW, QHIGH)):
                        sp.dma_start(stack_q[odd_m][DH * r:DH * (r + 1), c::HT],
                                     split_qk[DH * c:DH * (c + 1), slot]).then_inc(cq_stacked, 16)

        @block.sync
        def _(sp):
            sp.dma_start(rope_t[:], rope).then_inc(const_loaded, 16)
            for i, b in enumerate((sbq, sbk, cbq, cbkv[0:D], sbv, cbkv[D:2 * D])):
                sp.dma_start(b_rows[KD * i:KD * (i + 1)], b.rearrange("(m p) -> m p", p=P)).then_inc(const_loaded, 16)
            for dst, b in ((b_so, sbo), (b_cp, cbp)):
                sp.dma_start(dst[:], b.partition_broadcast(L)).then_inc(const_loaded, 16)
            sp.dma_start(g_bias[:], gb.partition_broadcast(P)).then_inc(const_loaded, 16)
            raw = flat32[:, 0:5 * KD * D].rearrange("p (w k f) -> p w k f", w=5, k=KD)
            sp.dma_start(raw[:, 0], sWq.rearrange("(k p) f -> p k f", p=P)).then_inc(raw_loaded[0], 16)
            sp.dma_start(raw[:, 1], sWk.rearrange("(k p) f -> p k f", p=P)).then_inc(raw_loaded[1], 16)
            load_x(sp, 0)
            sp.wait_ge(setup_done, 2)
            load_ctx(sp, 0)
            sp.dma_start(raw[:, 2], sWv.rearrange("(k p) f -> p k f", p=P)).then_inc(raw_loaded[2], 16)
            sp.dma_start(raw[:, 3], sWo.rearrange("(k p) f -> p k f", p=P)).then_inc(raw_loaded[3], 16)
            sp.dma_start(raw[:, 4], cWq.rearrange("(k p) f -> p k f", p=P)).then_inc(raw_loaded[4], 16)
            sp.wait_ge(wT_low, 8)
            sp.dma_start(raw[:, 0], cWp.rearrange("(k p) f -> p k f", p=P)).then_inc(raw2_loaded, 16)
            sp.wait_ge(wT_low, 16)
            sp.dma_start(flat32[:, KD * D:KD * D + KC * 2 * D].rearrange("p (k f) -> p k f", k=KC),
                         cWkv.rearrange("(k p) f -> p k f", p=P)).then_inc(raw2_loaded, 16)
            sp.wait_ge(w_low, 3)
            pipeline(sp, lambda it: sync_iteration(sp, it))
            ffn_sync(sp)

        def pe_chunk(pe, it, name):
            m = it.n + 1
            odd_m = not it.odd
            f = filler[it.bank(name)]
            done = it.done(name)
            if not (isinstance(done, int) and done <= 2):
                pe.wait_ge(chunk_out, done - 2)
            last = None
            kind, i = name[:2], int(name[2:]) if name[2:].isdigit() else 0
            if name in ("X1T", "X2T"):
                pe.wait_ge(norm_done, 2 * m + (1 if name == "X1T" else 2))
                for k in range(KD):
                    last = pe.transpose(f[:, k * L:(k + 1) * L], x_norm[:, k * P:(k + 1) * P], ident[0:L, 0:L])
            elif name in ("SQ", "SK", "CQ"):
                pe.wait_ge(chunk_out, it.done("X2T" if name == "CQ" else "X1T"))
                w = w_cross["q"] if name == "CQ" else w_self[name[1].lower()]
                for o in range(KD):
                    last = split3(pe, f[:, o * L:(o + 1) * L],
                                  [(lambda p, k=k: w[:, k, p, o * P:(o + 1) * P], lambda p, k=k: xT[:, p, k])
                                   for k in range(KD)])
            elif name == "SV":
                last = split3(pe, f[0:L, 0:D], [(lambda p, k=k: xT[:, p, k], lambda p, k=k: w_self["v"][:, k, p])
                                                for k in range(KD)])
            elif kind == "SS":
                pe.wait_ge(qk_stacked, 16 * 6 * HT * (m + 1))
                for j in range(4):
                    h = 4 * i + j
                    last = pe.matmul(f[0:L, j * L:(j + 1) * L], stack_qk[:, 1, h], stack_qk[:, 0, h],
                                     start=True, stop=True)
            elif kind == "SP":
                pe.wait_ge(s_exp, m + 1)
                for j in range(4):
                    last = pe.transpose(f[0:L, j * L:(j + 1) * L], s_sc[:, i, j * L:(j + 1) * L], ident[0:L, 0:L])
            elif name == "SO":
                pe.wait_ge(chunk_out, it.done("SP3"))
                for h in range(H):
                    def probs(p, h=h):
                        c = (p * 4 + h % 4) * L
                        return s_scT[:, h // 4, c:c + L]
                    last = split3(pe, f[0:L, h * DH:(h + 1) * DH],
                                  [(probs, lambda p, h=h: sv[:, p, h * DH:(h + 1) * DH])])
            elif name in ("OT", "TT"):
                if name == "OT":
                    pe.wait_ge(chunk_out, it.done("SO"))
                elif it.cross:
                    pe.wait_ge(pT_out, H * it.n + 1)
                else:
                    pe.wait_ge(c_out_done, 1)
                src = s_out if name == "OT" else c_out
                for k in range(KD):
                    last = pe.transpose(f[:, k * L:(k + 1) * L], src[:, k * P:(k + 1) * P], ident[0:L, 0:L])
            elif name in ("OP", "TP"):
                pe.wait_ge(chunk_out, it.done("OT" if name == "OP" else "TT"))
                w = w_self["o"] if name == "OP" else w_cross["p"]
                last = split3(pe, f[0:L, 0:D], [(lambda p, k=k: oT[:, p, k], lambda p, k=k: w[:, k, p])
                                                for k in range(KD)])
            elif kind == "CX":
                pe.wait_ge(ctx_loaded, 16 * 2 * (m + 1))
                k, hf = i // 2, i % 2
                for j in range(3):
                    last = pe.transpose(f[:, j * CW:(j + 1) * CW], c_raw[:, 3 * hf + j, k * P:(k + 1) * P],
                                        ident[0:CW, 0:CW])
            elif kind == "CK":
                pe.wait_ge(chunk_out, it.done("CX5"))
                o, hf = i // 2, i % 2
                last = split3(pe, f[:, 0:HC],
                              [(lambda p, k=k: w_kv[:, k, p, o * P:(o + 1) * P],
                                lambda p, k=k: cT[:, k, p, hf * HC:(hf + 1) * HC]) for k in range(KC)])
            elif kind == "CV":
                pe.wait_ge(chunk_out, it.done("CX5"))
                last = split3(pe, f[0:CW, 0:D],
                              [(lambda p, k=k: cT[:, k, p, i * CW:(i + 1) * CW],
                                lambda p, k=k: w_kv[:, k, p, D:2 * D]) for k in range(KC)])
            last.then_inc(chunk_ready, 1)

        def pe_scores(pe, n, odd, h):
            g = H * n + h
            if not (isinstance(g, int) and g < 2):
                pe.wait_ge(exp_done, g - 1)
            if h == 0:
                pe.wait_ge(k_stacked, 16 * 3 * HT * (n + 1))
                pe.wait_ge(cq_stacked, 16 * 3 * HT * (n + 1))
            for hf in range(2):
                last = pe.matmul(score[h % 2][0:L, hf, 0:HC], stack_q[odd][:, h],
                                 stack_k[odd][:, h, hf * HC:(hf + 1) * HC], start=True, stop=True)
            last.then_inc(score_ready, 1)

        def pe_head_out(pe, n, odd, h):
            pe.wait_ge(pT_out, H * n + h + 1)
            o = OCOL + DH * (h % 4)
            split3(pe, pT[0:L, 0, o:o + DH],
                   [(lambda p, t=t: probT[:, p, t * L:(t + 1) * L],
                     lambda p, t=t: cv[odd][:, p, t, h * DH:(h + 1) * DH]) for t in range(CT)])\
                .then_inc(head_done, 1)

        def pe_transpose_probs(pe, n, h):
            g = H * n + h
            pe.wait_ge(exp_done, g + 1)
            if not (isinstance(g, int) and g < 1):
                pe.wait_ge(pT_out, g)
            for t in range(CT):
                last = pe.transpose(pT[0:CW, t // 3, (t % 3) * L:(t % 3 + 1) * L],
                                    prob[h % 2][:, t * CW:(t + 1) * CW], ident[0:L, 0:L])
            last.then_inc(pT_ready, 1)

        def pe_iteration(pe, it):
            n = it.n
            begun = not (isinstance(n, int) and n <= 0)
            for h in range(H):
                if it.cross and h + 1 < H:
                    pe_scores(pe, n, it.odd, h + 1)
                elif h + 1 == H and it.prep:
                    pe_scores(pe, n + 1, not it.odd, 0)
                for name in it.steps[h]:
                    pe_chunk(pe, it, name)
                if h == 0 and begun:
                    pe_head_out(pe, n - 1, not it.odd, H - 1)
                elif h > 0 and it.cross:
                    pe_head_out(pe, n, it.odd, h - 1)
                if it.cross:
                    pe_transpose_probs(pe, n, h)

        @block.tensor
        def _(pe):
            pe.wait_ge(ident_done, 2)
            pe.wait_ge(const_loaded, 16 * 10)
            pe.transpose(psum[:, 7, 0:6 * KD], b_rows[:], ident[0:6 * KD, 0:6 * KD]).then_inc(bias_ready_T, 1)
            raw = flat32[:, 0:5 * KD * D].rearrange("p (w k f) -> p w k f", w=5, k=KD)
            for i in range(4 * KD):
                w, k = i // KD, i % KD
                pe.wait_ge(raw_loaded[w], 16)
                if i == 7:
                    pe.wait_ge(bias_done, 1)
                if i >= 8:
                    pe.wait_ge(wT_low, i - 7)
                for o in range(KD):
                    last = pe.transpose(psum[:, i % 8, o * P:(o + 1) * P], raw[:, w, o, k * P:(k + 1) * P], ident[:])
                last.then_inc(wT_ready, 1)
            pe.wait_ge(wT_low, 4 * KD)
            pe.wait_ge(w_low, 3)
            pe.wait_ge(setup_done, 3)
            pe.wait_ge(bv_split, 1)
            for i, w in enumerate((w_self["o"], w_cross["p"])):
                split3(pe, psum[0:L, 6 + i, 0:D],
                       [(lambda p, k=k: b_value[:, i, p, k:k + 1].to_broadcast([P, L]), lambda p, k=k: w[:, k, p])
                        for k in range(KD)]).then_inc(bv_ready, 1)
            pe.wait_ge(bv_folded, 2)
            pipeline(pe, lambda it: pe_iteration(pe, it))
            ffn_tensor(pe)

        def act_chunk(act, it, name):
            if name not in SPLIT:
                return
            f = filler[it.bank(name)]
            act.wait_ge(chunk_ready, it.done(name))
            kind, i = name[:2], int(name[2:]) if name[2:].isdigit() else 0
            if name in ("X1T", "X2T", "OT", "TT"):
                dst = (xT if name[0] == "X" else oT)[:, 0].rearrange("p k l -> p (k l)")
                op = act.activation(dst, f[:, 0:KD * L], ACT.Copy)
            elif name == "SV":
                op = act.activation(sv[:, 0], f[0:L, 0:D], ACT.Copy)
            elif kind == "SP":
                if i == 0:
                    act.wait_ge(s_sum_done, it.n + 2)
                op = act.activation(s_scT[:, i, 0:4 * L], f[0:L, 0:4 * L], ACT.Copy)
            elif kind == "CX":
                op = act.activation(cT[:, i // 2, 0, (i % 2) * HP:(i % 2 + 1) * HP], f[:, 0:HP], ACT.Copy)
            elif kind == "CK":
                if i == 0 and not (isinstance(it.n, int) and it.n < 0):
                    act.wait_ge(k_stacked, 16 * 3 * HT * (it.n + 1))
                op = act.activation(split_k[:, 0, i // 2, (i % 2) * HC:(i % 2 + 1) * HC], f[:, 0:HC],
                                    ACT.Identity, bias=b_part[:, 3, i // 2:i // 2 + 1])
            elif kind == "CV":
                op = act.activation(cv[not it.odd][:, 0, i], f[0:CW, 0:D], ACT.Copy)
            op.then_inc(chunk_high, 1)

        def act_exp(act, n, odd, h):
            act.wait_ge(bias_ready, H * n + h + 1)
            act.activation(prob[h % 2][:, 0:LC].rearrange("q (a k) -> q a k", a=2), score[h % 2][0:L, :, 0:HC],
                           ACT.Exp, bias=c_bias[:, int(odd), h:h + 1], scale=SOFT,
                           accum_out=c_sum[:, int(odd), h:h + 1]).then_inc(exp_done, 1)

        def act_probs_high(act, n, h):
            act.wait_ge(pT_ready, H * n + h + 1)
            act.activation(probT[:, 0].rearrange("k (a c) -> k a c", a=2), pT[0:CW, :, 0:3 * L], ACT.Copy)\
               .then_inc(pT_high, 1)

        def act_iteration(act, it):
            n = it.n
            for h in range(H):
                if it.cross and h > 0:
                    act_probs_high(act, n, h - 1)
                elif h == 0 and not (isinstance(n, int) and n <= 0):
                    act_probs_high(act, n - 1, H - 1)
                for name in it.steps[h][:1]:
                    act_chunk(act, it, name)
                if it.cross and h + 1 < H:
                    act_exp(act, n, it.odd, h + 1)
                elif h + 1 == H and it.prep:
                    act_exp(act, n + 1, not it.odd, 0)
                for name in it.steps[h][1:]:
                    act_chunk(act, it, name)
                if h == 6 and it.prep:
                    act.wait_ge(s_shifted, n + 2)
                    act.activation(s_sc[:, :, :], s_sc[:, :, :], ACT.Exp, scale=SOFT).then_inc(s_exp, 1)

        @block.scalar
        def _(act):
            raw = flat32[:, 0:5 * KD * D].rearrange("p (w k f) -> p w k f", w=5, k=KD)
            for i in range(4 * KD):
                act.wait_ge(wT_ready, i + 1)
                act.activation(w_self["qkvo"[i // KD]][:, i % KD, 0], psum[:, i % 8], ACT.Copy, scale=WSCALE)\
                   .then_inc(wT_high, 1)
            act.wait_ge(raw_loaded[4], 16)
            act.activation(w_cross["q"][:, :, 0], raw[:, 4], ACT.Copy, scale=WSCALE).then_inc(w_high, 1)
            act.wait_ge(raw2_loaded, 16 * 2)
            act.activation(w_cross["p"][:, :, 0], raw[:, 0], ACT.Copy, scale=WSCALE).then_inc(w_high, 1)
            kv = flat32[:, KD * D:KD * D + KC * 2 * D].rearrange("p (k f) -> p k f", k=KC)
            act.activation(w_kv[:, :, 0], kv, ACT.Copy, scale=WSCALE).then_inc(w_high, 1)
            act.wait_ge(bias_done, 1)
            pipeline(act, lambda it: act_iteration(act, it))
            ffn_scalar(act)

        def dve_chunk(dve, it, name):
            n, m = it.n, it.n + 1
            odd_m = not it.odd
            f = filler[it.bank(name)]
            kind, i = name[:2], int(name[2:]) if name[2:].isdigit() else 0
            if name in SPLIT:
                dve.wait_ge(chunk_high, it.high_done(name))
            else:
                dve.wait_ge(chunk_ready, it.done(name))

            def low(dst, src, high):
                return dve.tensor_tensor(dst, src, high, ALU.subtract)

            if name in ("X1T", "X2T", "OT", "TT"):
                d = xT if name[0] == "X" else oT
                op = low(d[:, 1].rearrange("p k l -> p (k l)"), f[:, 0:KD * L], d[:, 0].rearrange("p k l -> p (k l)"))
            elif name in ("SQ", "SK"):
                if not (isinstance(n, int) and n < 0):
                    dve.wait_ge(cq_split, m) if name == "SQ" else dve.wait_ge(qk_split, 2 * m)
                op = dve.tensor_tensor((tmp_q if name == "SQ" else tmp_k)[:],
                                       f[:, 0:KD * L].rearrange("p (k l) -> p k l", k=KD),
                                       b_part[:, int(name == "SK")].unsqueeze(2).to_broadcast([P, KD, L]), ALU.add)
            elif name == "CQ":
                dve.wait_ge(qk_split, 2 * m + 1)
                op = dve.tensor_tensor(tmp_q[:], f[:, 0:KD * L].rearrange("p (k l) -> p k l", k=KD),
                                       b_part[:, 2].unsqueeze(2).to_broadcast([P, KD, L]), ALU.add)
            elif name == "SV":
                op = low(sv[:, 1], f[0:L, 0:D], sv[:, 0])
            elif kind == "SS":
                op = dve.tensor_tensor(s_sc[:, i].rearrange("q (j k) -> q j k", j=4),
                                       f[0:L, 0:4 * L].rearrange("q (j k) -> q j k", j=4),
                                       mask[:].unsqueeze(1).to_broadcast([L, 4, L]), ALU.add)
            elif kind == "SP":
                op = low(s_scT[:, i, 4 * L:8 * L], f[0:L, 0:4 * L], s_scT[:, i, 0:4 * L])
            elif name == "SO":
                dve.wait_ge(s_rinv_done, m + 1)
                op = dve.tensor_tensor(s_out[:].rearrange("q (h d) -> q h d", h=H),
                                       f[0:L, 0:D].rearrange("q (h d) -> q h d", h=H),
                                       s_rinv[:].unsqueeze(2).to_broadcast([L, H, DH]), ALU.mult)
            elif name == "OP":
                dve.wait_ge(x_biased, 2 * m + 1)
                if not (isinstance(n, int) and n < 1):
                    dve.wait_ge(x2_stored, 16 * n)
                op = dve.scalar_tensor_tensor(x_mid[odd_m][:], f[0:L, 0:D], PSCALE, x_in[:], ALU.mult, ALU.add)
            elif name == "TP":
                buf = x_mid[not it.odd]
                dve.wait_ge(x_biased, 2 * n)
                op = dve.scalar_tensor_tensor(buf[:], f[0:L, 0:D], PSCALE, buf[:], ALU.mult, ALU.add)
            elif kind == "CX":
                c = slice((i % 2) * HP, (i % 2 + 1) * HP)
                op = low(cT[:, i // 2, 1, c], f[:, 0:HP], cT[:, i // 2, 0, c])
            elif kind == "CK":
                c = slice((i % 2) * HC, (i % 2 + 1) * HC)
                op = dve.scalar_tensor_tensor(split_k[:, 1, i // 2, c], f[:, 0:HC], b_part[:, 3, i // 2:i // 2 + 1],
                                              split_k[:, 0, i // 2, c], ALU.add, ALU.subtract)
            elif kind == "CV":
                op = low(cv[odd_m][:, 1, i], f[0:CW, 0:D], cv[odd_m][:, 0, i])
            op.then_inc(chunk_out, 1)

        def dve_max(dve, n, odd, h):
            g = H * n + h
            dve.wait_ge(score_ready, g + 1)
            if not (isinstance(g, int) and g < 2 * H):
                dve.wait_ge(exp_done, g - H)
            dve.tensor_reduce(c_max[:, int(odd), h:h + 1], score[h % 2][0:L, :, 0:HC], AXIS.XY, ALU.max)\
               .then_inc(max_done, 1)
            dve.wait_ge(max_done, g + 1)
            dve.tensor_scalar(c_bias[:, int(odd), h:h + 1], c_max[:, int(odd), h:h + 1], -SOFT, None, ALU.mult)\
               .then_inc(bias_ready, 1)

        def dve_probs_low(dve, n, h):
            dve.wait_ge(pT_high, H * n + h + 1)
            return dve.tensor_tensor(probT[:, 1].rearrange("k (a c) -> k a c", a=2), pT[0:CW, :, 0:3 * L],
                                     probT[:, 0].rearrange("k (a c) -> k a c", a=2), ALU.subtract)

        def dve_inverse(dve, n, odd, group):
            dve.wait_ge(exp_done, H * n + 4 * group + 4)
            s = slice(4 * group, 4 * group + 4)
            dve.reciprocal(c_rinv[:, int(odd), s], c_sum[:, int(odd), s]).then_inc(c_rinv_done, 1)

        def dve_heads_out(dve, n, odd, group):
            dve.wait_ge(c_rinv_done, 4 * n + group + 1)
            dve.wait_ge(head_done, H * n + 4 * group + 4)
            s = slice(4 * group, 4 * group + 4)
            return dve.tensor_tensor(c_out[:, 4 * DH * group:4 * DH * (group + 1)].rearrange("q (h d) -> q h d", h=4),
                                     pT[0:L, 0, OCOL:OCOL + 4 * DH].rearrange("q (h d) -> q h d", h=4),
                                     c_rinv[:, int(odd), s].unsqueeze(2).to_broadcast([L, 4, DH]), ALU.mult)

        def dve_stats(dve, src, count):
            if not (isinstance(count, int) and count < 1):
                dve.wait_ge(ln_shift, 2 * count)
            dve.bn_stats(stats[0:L], src).then_inc(bn_done, 1)
            wait_alone(dve, bn_done, count + 1)
            dve.bn_aggr(moments[0:L], stats[0:L]).then_inc(stats_done, 1)

        def dve_iteration(dve, it):
            n, m = it.n, it.n + 1
            begun = not (isinstance(n, int) and n <= 0)
            for h in range(H):
                if it.cross and h + 1 < H:
                    dve_max(dve, n, it.odd, h + 1)
                elif h + 1 == H and it.prep:
                    dve_max(dve, n + 1, not it.odd, 0)
                if h == 0 and begun:
                    dve_inverse(dve, n - 1, not it.odd, 3)
                    dve_probs_low(dve, n - 1, H - 1).then_inc(pT_out, 1)
                    if not it.cross:
                        dve_heads_out(dve, n - 1, not it.odd, 3).then_inc(c_out_done, 1)
                elif h > 0 and it.cross:
                    if (h - 1) % 4 == 0 and (h > 1 or begun):
                        if h > 1:
                            dve_inverse(dve, n, it.odd, (h - 1) // 4 - 1)
                        dve_probs_low(dve, n, h - 1).then_inc(pT_low, 1)
                        if h > 1:
                            dve_heads_out(dve, n, it.odd, (h - 1) // 4 - 1).then_inc(pT_out, 1)
                        else:
                            dve_heads_out(dve, n - 1, not it.odd, 3).then_inc(pT_out, 1)
                    else:
                        dve_probs_low(dve, n, h - 1).then_inc(pT_out, 1)
                if h == 7 and it.prep:
                    dve.wait_ge(s_exp, m + 1)
                    dve.tensor_reduce(s_sum[:], s_sc.rearrange("q g (j k) -> q (g j) k", j=4), AXIS.X, ALU.add)\
                       .then_inc(s_sum_done, 1)
                    dve.wait_ge(s_sum_done, m + 1)
                    dve.reciprocal(s_rinv[:], s_sum[:]).then_inc(s_rinv_done, 1)
                for name in it.steps[h]:
                    dve_chunk(dve, it, name)
                    if name == "SS3":
                        dve.wait_ge(chunk_out, it.done("SS3"))
                        dve.tensor_reduce(s_max[:], s_sc.rearrange("q g (j k) -> q (g j) k", j=4), AXIS.X, ALU.max)\
                           .then_inc(s_max_done, 1)
                    if name == "OP":
                        dve.wait_ge(chunk_out, it.done("OP"))
                        dve_stats(dve, x_mid[not it.odd][:], 2 * m + 1)
                if h == H - 1 and it.prep and not (isinstance(n, int) and n == B - 2):
                    dve.wait_ge(x_loaded, 16 * (n + 3))
                    dve_stats(dve, x_in[:], 2 * m + 2)

        @block.vector
        def _(dve):
            raw = flat32[:, 0:5 * KD * D].rearrange("p (w k f) -> p w k f", w=5, k=KD)
            dve.memset(ident[:], 0.0).then_inc(ident_done, 1)
            dve.memset(mask[:], 0.0).then_inc(setup_done, 1)
            dve.memset(c_raw[96:CW, CT - 1], 0.0).then_inc(setup_done, 1)
            for i in range(2):
                last = dve.memset(prob[i][:, LC:LCP], 0.0)
            last.then_inc(setup_done, 1)
            dve.memset(half[:], -0.5).then_inc(setup_done, 1)
            for e in range(E):
                dve.memset(rank[:, e:e + 1], float(E - e)).then_inc(rank_set, 1)
            dve.wait_ge(bias_ready_T, 1)
            dve.tensor_scalar(b_part[:].rearrange("p b k -> p (b k)"), psum[:, 7, 0:6 * KD], WSCALE, None, ALU.mult)\
               .then_inc(bias_done, 1)
            dve.wait_ge(bias_done, 1)
            dve.tensor_copy(b_value[:, :, 0], b_part[:, 4:6]).then_inc(bv_high, 1)
            dve.wait_ge(bv_high, 1)
            dve.tensor_tensor(b_value[:, :, 1], b_part[:, 4:6], b_value[:, :, 0], ALU.subtract).then_inc(bv_split, 1)
            dve.wait_ge(x_loaded, 16)
            dve_stats(dve, x_in[:], 0)
            for i in range(4 * KD):
                dve.wait_ge(wT_high, i + 1)
                w = w_self["qkvo"[i // KD]]
                dve.scalar_tensor_tensor(w[:, i % KD, 1], psum[:, i % 8], WSCALE, w[:, i % KD, 0],
                                         ALU.mult, ALU.subtract).then_inc(wT_low, 1)
            kv = flat32[:, KD * D:KD * D + KC * 2 * D].rearrange("p (k f) -> p k f", k=KC)
            for i, (w, src) in enumerate(((w_cross["q"], raw[:, 4]), (w_cross["p"], raw[:, 0]), (w_kv, kv))):
                dve.wait_ge(w_high, i + 1)
                dve.scalar_tensor_tensor(w[:, :, 1], src, WSCALE, w[:, :, 0], ALU.mult, ALU.subtract)\
                   .then_inc(w_low, 1)
            dve.wait_ge(setup_done, 5)
            for i, b in enumerate((b_so, b_cp)):
                dve.wait_ge(bv_ready, i + 1)
                dve.scalar_tensor_tensor(b[:], psum[0:L, 6 + i, 0:D], PSCALE, b[:], ALU.mult, ALU.add)\
                   .then_inc(bv_folded, 1)
            pipeline(dve, lambda it: dve_iteration(dve, it))
            ffn_vector(dve)

        def pool_norm(pool, src, count, x_bias):
            wait_alone(pool, stats_done, count + 1)
            pool.tensor_scalar(shift[0:L, 0:1], moments[0:L, 0:1], -1.0, None, ALU.mult).then_inc(ln_shift, 1)
            pool.tensor_scalar(shift[0:L, 1:2], moments[0:L, 1:2], EPS, None, ALU.add).then_inc(ln_shift, 1)
            pool.wait_ge(ln_shift, 2 * count + 2)
            pool.tensor_tensor(rstd[0:L], shift[0:L, 1:2], half[0:L], ALU.pow).then_inc(ln_rstd, 1)
            wait_alone(pool, ln_rstd, count + 1)
            pool.tensor_scalar(x_norm[:], src, shift[0:L, 0:1], rstd[0:L, 0:1], ALU.add, ALU.mult)\
                .then_inc(norm_done, 1)
            pool.wait_ge(norm_done, count + 1)
            pool.tensor_tensor(src, src, x_bias[:], ALU.add).then_inc(x_biased, 1)

        def pool_split_q(pool, count):
            pool.tensor_copy(split_qk[:, QHIGH], tmp_q[:]).then_inc(cq_high, 1)
            pool.wait_ge(cq_high, count + 1)
            return pool.tensor_tensor(split_qk[:, QLOW], tmp_q[:], split_qk[:, QHIGH], ALU.subtract)

        def pool_iteration(pool, it):
            n, m = it.n, it.n + 1
            begun = not (isinstance(n, int) and n <= 0)
            if it.prep:
                for i, name in enumerate(("SQ", "SK")):
                    tmp = (tmp_q, tmp_k)[i]
                    pool.wait_ge(chunk_out, it.done(name))
                    pool.tensor_tensor(tmp[:], tmp[:], rope_t[:].unsqueeze(1).to_broadcast([P, KD, L]), ALU.mult)\
                        .then_inc(qk_rotated, 1)
                    if i == 0 and not (isinstance(n, int) and n < 0):
                        pool.wait_ge(qk_stacked, 16 * 6 * HT * m)
                        pool.wait_ge(cq_stacked, 16 * 3 * HT * m)
                    wait_alone(pool, qk_rotated, 2 * m + i + 1)
                    if i == 0:
                        pool_split_q(pool, 2 * m).then_inc(qk_split, 1)
                    else:
                        pool.tensor_copy(split_qk[:, KHIGH], tmp_k[:]).then_inc(qk_high, 1)
                        pool.wait_ge(qk_high, m + 1)
                        pool.tensor_tensor(split_qk[:, KLOW], tmp_k[:], split_qk[:, KHIGH], ALU.subtract)\
                            .then_inc(qk_split, 1)
            if it.prep:
                pool.wait_ge(s_max_done, m + 1)
                for g in range(2):
                    last = pool.tensor_tensor(s_sc[:, 2 * g:2 * g + 2].rearrange("q g (j k) -> q (g j) k", j=4),
                                              s_sc[:, 2 * g:2 * g + 2].rearrange("q g (j k) -> q (g j) k", j=4),
                                              s_max[:, 8 * g:8 * g + 8].unsqueeze(2).to_broadcast([L, 8, L]),
                                              ALU.subtract)
                last.then_inc(s_shifted, 1)
                pool_norm(pool, x_mid[not it.odd][:], 2 * m + 1, b_cp)
                pool.wait_ge(chunk_out, it.done("CQ"))
                wait_alone(pool, qk_stacked, 16 * 6 * HT * (m + 1))
                pool_split_q(pool, 2 * m + 1).then_inc(cq_split, 1)
                if not (isinstance(n, int) and n == B - 2):
                    pool_norm(pool, x_in[:], 2 * m + 2, b_so)

        @block.gpsimd
        def _(pool):
            pool.wait_ge(ident_done, 1)
            pool.affine_select(out=ident[:], in_=ident[:], compare_op=ALU.not_equal, fill=1.0, base=0,
                               pattern=[[-1, P]], channel_multiplier=1).then_inc(ident_done, 1)
            pool.wait_ge(setup_done, 4)
            pool.affine_select(out=mask[:], in_=mask[:], compare_op=ALU.is_ge, fill=MASKED, base=0,
                               pattern=[[-1, L]], channel_multiplier=1).then_inc(setup_done, 1)
            pool.wait_ge(bv_folded, 2)
            pool_norm(pool, x_in[:], 0, b_so)
            pipeline(pool, lambda it: pool_iteration(pool, it))
            ffn_gpsimd(pool)


_INS = ["x", "ctx_768", "L0_attn_Wq", "L0_attn_bq", "L0_attn_Wk", "L0_attn_bk", "L0_attn_Wv", "L0_attn_bv",
        "L0_attn_Wo", "L0_attn_bo", "L0_xattn_q_w", "L0_xattn_q_b", "L0_xattn_kv_w", "L0_xattn_kv_b",
        "L0_xattn_proj_w", "L0_xattn_proj_b", "L0_ffn_gate_w", "L0_ffn_gate_b", "L0_ffn_expert_w",
        "L0_ffn_expert_b"]


def rotation_table():
    i = np.arange(DH // 2, dtype=np.float32)
    theta = np.arange(L, dtype=np.float32)[None, :] * np.power(np.float32(10000.0), -2.0 * i / DH,
                                                               dtype=np.float32)[:, None]
    both = (np.cos(theta) + np.sin(theta)).astype(np.float32)
    return np.ascontiguousarray(np.tile(both, (2 * HT, 1)))


def kernel(**inputs):
    import concourse.bacc as bacc
    from concourse.bass_utils import run_bass_kernel_spmd

    nc = bacc.Bacc("TRN2", target_bir_lowering=False, num_devices=1)
    arrays, args = {}, []
    for name in _INS:
        a = np.ascontiguousarray(inputs[name])
        arrays[f"in_{name}"] = a
        args.append(nc.dram_tensor(f"in_{name}", a.shape, mybir.dt.from_np(a.dtype), kind="ExternalInput").ap())
    arrays["in_rotation"] = rotation_table()
    args.append(nc.dram_tensor("in_rotation", (P, L), F32, kind="ExternalInput").ap())
    args.append(nc.dram_tensor("x2_scratch", (B, L, D), F32, kind="Internal").ap())
    args.append(nc.dram_tensor("out_0", (B, L, D), F32, kind="ExternalOutput").ap())
    build_layer(nc, *args)
    return run_bass_kernel_spmd(nc, [arrays], core_ids=[0]).results[0]["out_0"]
```

```python
from contextlib import ExitStack

import concourse.bass as bass
import numpy as np
from concourse import mybir

F32 = mybir.dt.float32
F16 = mybir.dt.float16
ALU = mybir.AluOpType
ACT = mybir.ActivationFunctionType
AXIS = mybir.AxisListType

P = 128
B, L, D = 16, 100, 512
LC, DC = 722, 384
H, DH = 16, 32
E = 8
T = B * L
KD, KC = D // P, DC // P
HT = P // DH
CT = 6
CW = 121
LCP = CT * CW
HC = LC // 2
HP = LCP // 2
TT = (T + P - 1) // P
TLAST = T - (TT - 1) * P
WSCALE = 32.0
PSCALE = 1.0 / (WSCALE * WSCALE)
SOFT = PSCALE / float(np.sqrt(DH))
EPS = 1e-5
MASKED = -1e30
BANK = 512
OCOL = 304
KLOW, KHIGH, QLOW, QHIGH = range(4)

STEP_CHUNKS = [
    ["X1T", "CX0", "SQ"],
    ["CX1", "SK"],
    ["CX2", "CX3", "SV"],
    ["CX4", "CX5", "TT"],
    ["SS0", "SS1", "TP"],
    ["SS2", "SS3", "CK0"],
    ["CV0", "CK1"],
    ["SP0", "SP1", "CK2"],
    ["SP2", "SP3", "CK3"],
    ["SO0", "SO1", "CK4"],
    ["OT", "CK5", "OP"],
    ["CK6", "CK7"],
    ["X2T", "CV1", "CQ"],
    ["CV2", "CV3"],
    ["CV4"],
    ["CV5"],
]
EXP_STEPS = (5, 6)
SUM_STEPS = (6, 7)
PE_ORDER = "S0OT123"
ACT_ORDER = "0PE123"
DVE_ORDER = "M0L123"
SPLIT = ("X1T", "SV", "SP0", "SP1", "SP2", "SP3", "OT", "X2T", "TT") + tuple(
    [f"CX{c}" for c in range(6)] + [f"CK{c}" for c in range(8)] + [f"CV{c}" for c in range(6)])


class Iteration:

    def __init__(self, n, odd, cross=True, prep=True, tail=True):
        self.n, self.odd, self.cross, self.prep, self.tail = n, odd, cross, prep, tail
        self.steps = [[c for c in step if (tail if c in ("TT", "TP") else prep)] for step in STEP_CHUNKS]
        self.order = [c for step in self.steps for c in step]

    @staticmethod
    def _count(names):
        return len(names), sum(c in SPLIT for c in names)

    def _before(self, which):
        every = [c for step in STEP_CHUNKS for c in step]
        head = self._count([c for c in every if c not in ("TT", "TP")])[which]
        each = self._count(every)[which]
        if isinstance(self.n, int):
            return 0 if self.n < 0 else head if self.n == 0 else (
                2 * head + (min(self.n, B - 1) - 1) * each + (self.n - B + 1 > 0) * self._count(["TT", "TP"])[which])
        return 2 * head + (self.n - 1) * each

    def bank(self, chunk):
        every = sum(len(s) for s in STEP_CHUNKS)
        head = every - 2
        if isinstance(self.n, int):
            start = self._before(0)
        else:
            start = 2 * head + (0 if self.odd else every)
        return (start + self.order.index(chunk)) % 2

    def done(self, chunk):
        return self._before(0) + self.order.index(chunk) + 1

    def high_done(self, chunk):
        return self._before(1) + sum(c in SPLIT for c in self.order[:self.order.index(chunk) + 1])

    def all_before(self):
        return self._before(0)


def build_layer(nc, x, ctx, sWq, sbq, sWk, sbk, sWv, sbv, sWo, sbo, cWq, cbq, cWkv, cbkv, cWp, cbp,
                gW, gb, eW, eb, rope, x2_dram, out):
    with ExitStack() as stack:
        def sb(name, shape, dt=F32):
            return stack.enter_context(nc.sbuf_tensor(name, shape, dt))

        def sem(name):
            return stack.enter_context(nc.semaphore(name))

        w_self_all = sb("w_self_all", [P, 4, KD, 2, D], F16)
        w_self = {k: w_self_all[:, i] for i, k in enumerate("qkvo")}
        w_cross = {k: sb(f"w_cross_{k}", [P, KD, 2, D], F16) for k in "qp"}
        w_kv = sb("w_kv", [P, KC, 2, 2 * D], F16)
        ident = sb("ident", [P, P])
        mask = sb("mask", [L, L])
        rope_t = sb("rope_t", [P, L])
        b_part = sb("b_part", [P, 6, KD])
        b_rows = sb("b_rows", [6 * KD, P])
        b_value = sb("b_value", [P, 2, 2, KD], F16)
        b_so, b_cp = sb("b_so", [L, D]), sb("b_cp", [L, D])
        half = sb("half", [P, 1])
        x_in = sb("x_in", [L, D])
        x_norm = sb("x_norm", [L, D])
        s_out = x_norm
        x_mid = [sb(f"x_mid{i}", [L, D]) for i in range(2)]
        xT = sb("xT", [P, 2, KD, L], F16)
        stats = sb("stats", [P, 6])
        moments = sb("moments", [P, 2])
        shift = sb("shift", [P, 2])
        rstd = sb("rstd", [P, 1])
        tmp_q, tmp_k = sb("tmp_q", [P, KD, L]), sb("tmp_k", [P, KD, L])
        split_qk = sb("split_qk", [P, 4, KD, L], F16)
        stack_q = [sb(f"stack_q{i}", [3 * DH, H, L], F16) for i in range(2)]
        sv = sb("sv", [L, H, 2, DH], F16)
        c_raw = sb("c_raw", [CW, CT, DC])
        c_flat = c_raw[:].rearrange("p t c -> p (t c)")
        s_sc = c_flat[0:L, 0:H * L].rearrange("q (g c) -> q g c", g=4)
        s_scT = s_sc.bitcast(F16)
        s_max, s_sum, s_rinv = sb("s_max", [L, H]), sb("s_sum", [L, H]), sb("s_rinv", [L, H])
        oT = xT
        cT = sb("cT", [P, KC, 2, LCP], F16)
        split_k = sb("split_k", [P, 2, KD, LC], F16)
        cv = [sb(f"cv{i}", [CW, CT, H, 2, DH], F16) for i in range(2)]
        prob = [sb(f"prob{i}", [L, LCP]) for i in range(2)]
        probT = sb("probT", [CW, 2, CT * L], F16)
        c_max, c_bias, c_sum = (sb(n, [L, 2, H]) for n in ("c_max", "c_bias", "c_sum"))
        c_rinv = sb("c_rinv", [L, H])
        c_out = sb("c_out", [L, D])
        arena = sb("arena", [P, 2, H, LC], F16)
        stack_k = [arena[0:3 * DH, i] for i in range(2)]
        flat32 = arena[:].rearrange("p a h c -> p (a h c)").bitcast(F32)

        psum = stack.enter_context(nc.psum_tensor("psum", [P, 8, BANK], F32))
        score = [psum[:, 2 * i:2 * i + 2] for i in range(2)]
        pT = psum[:, 4:6]
        filler = [psum[:, 6], psum[:, 7]]

        const_loaded, setup_done, ident_done = sem("const_loaded"), sem("setup_done"), sem("ident_done")
        bias_ready_T, bias_done = sem("bias_ready_T"), sem("bias_done")
        raw_loaded = [sem(f"raw_loaded{i}") for i in range(5)]
        raw2_loaded = sem("raw2_loaded")
        wT_ready, wT_high, wT_low = sem("wT_ready"), sem("wT_high"), sem("wT_low")
        w_high, w_low = sem("w_high"), sem("w_low")
        x_loaded, ctx_loaded = sem("x_loaded"), sem("ctx_loaded")
        chunk_ready, chunk_high, chunk_out = sem("chunk_ready"), sem("chunk_high"), sem("chunk_out")
        bn_done, stats_done, ln_shift, ln_rstd, norm_done = (
            sem(n) for n in ("bn_done", "stats_done", "ln_shift", "ln_rstd", "norm_done"))
        x_biased = sem("x_biased")
        qk_rotated, qk_high, qk_split = (sem(n) for n in ("qk_rotated", "qk_high", "qk_split"))
        cq_high, cq_split = sem("cq_high"), sem("cq_split")
        s_max_done, s_shifted, s_exp, s_sum_done, s_rinv_done, s_out_done = (
            sem(n) for n in ("s_max_done", "s_shifted", "s_exp", "s_sum_done", "s_rinv_done", "s_out_done"))
        cq_stacked = [sem(f"cq_stacked{c}") for c in range(HT)]
        k_stacked = [sem(f"k_stacked{c}") for c in range(HT)]
        score_ready, max_done, bias_ready, exp_done = (
            sem(n) for n in ("score_ready", "max_done", "bias_ready", "exp_done"))
        pT_ready, pT_high, pT_low, pT_out, head_done = (
            sem(n) for n in ("pT_ready", "pT_high", "pT_low", "pT_out", "head_done"))
        c_rinv_done, c_summed, c_out_done = sem("c_rinv_done"), sem("c_summed"), sem("c_out_done")
        bv_high, bv_split, bv_ready, bv_folded = (sem(n) for n in ("bv_high", "bv_split", "bv_ready", "bv_folded"))
        x2_stored = sem("x2_stored")

        wait_over = sem("wait_over")

        def wait_alone(engine, semaphore, value):
            engine.wait_ge(semaphore, value)
            if not isinstance(value, int):
                engine.sem_inc(wait_over, 1)

        def split3(pe, out_ap, pairs):
            last = None
            for i, (a, b) in enumerate(pairs):
                for j, (pa, pb) in enumerate(((0, 0), (0, 1), (1, 0))):
                    last = pe.matmul(out_ap, a(pa), b(pb), start=(i == 0 and j == 0),
                                     stop=(i == len(pairs) - 1 and j == 2))
            return last

        xT3 = arena[:].rearrange("p a h c -> p (a h c)")[:, 0:2 * KD * TT * P]\
            .rearrange("p (s k t) -> p s k t", s=2, k=KD)
        raw_e = [flat32[:, KD * TT * P + i * KD * D:KD * TT * P + (i + 1) * KD * D]
                 .rearrange("p (o h) -> p o h", o=KD) for i in range(2)]
        self32 = w_self_all[:].rearrange("p w k s f -> p (w k s f)").bitcast(F32)
        y = self32[:, 0:TT * D].rearrange("p (t d) -> p t d", t=TT)
        y_norm = [self32[:, (TT + i) * D:(TT + i + 1) * D] for i in range(2)]
        wT_e = [w_cross["q"], w_cross["p"]]
        stats3, moments3 = sb("stats3", [P, 2, 6]), sb("moments3", [P, TT, 2])
        rstd3, nmean3 = sb("rstd3", [P, TT]), sb("nmean3", [P, TT])
        g_raw, g_T, g_bias = x_in[0:E], sb("g_T", [P, 2, KD, E], F16), sb("g_bias", [P, E])
        k_flat = split_k[:].rearrange("p s k c -> p (s k c)").bitcast(F32)
        gates, picked, first, tie, g_scaled = (
            k_flat[:, i * TT * E:(i + 1) * TT * E].rearrange("p (t e) -> p t e", e=E) for i in range(5))
        rank = sb("rank", [P, E])
        best = sb("best", [P, TT])
        g_now = sb("g_now", [P, 2, TT])
        gT_tok = c_flat[0:E, 0:TT * P].rearrange("e (t p) -> e t p", t=TT)
        e_bias = c_flat[0:E, TT * P:TT * P + D]

        y_zeroed, g_loaded = sem("y_zeroed"), sem("g_loaded")
        y_loaded = [sem(f"y_loaded{t}") for t in range(TT)]
        e_loaded = [sem(f"e_loaded{i}") for i in range(2)]
        f_bn, f_stats, f_half, f_rstd, f_norm = (sem(n) for n in ("f_bn", "f_stats", "f_half", "f_rstd", "f_norm"))
        f_T, f_high, f_low = sem("f_T"), sem("f_high"), sem("f_low")
        gT_ready, gT_high, gT_low = sem("gT_ready"), sem("gT_high"), sem("gT_low")
        logits_ready, route, g_exp = sem("logits_ready"), sem("route"), sem("g_exp")
        tokT_ready, tokT_out, eb_ready, eb_out = (sem(n) for n in ("tokT_ready", "tokT_out", "eb_ready", "eb_out"))
        e_T, e_high, e_low = sem("e_T"), sem("e_high"), sem("e_low")
        g_now_set, y_ready, y_done, y_stored = (sem(n) for n in ("g_now_set", "y_ready", "y_done", "y_stored"))
        rank_set = sem("rank_set")

        last_it = Iteration(B, False, cross=False, prep=False)
        ALL_CHUNKS = last_it.all_before() + 2
        ROUTED = 21

        def experts(engine, body):
            body(0, 0, 0, True)
            with engine.Fori(0, (E - 4) // 2) as i:
                body(2 * i + 1, 1, i, True)
                body(2 * i + 2, 0, i + 1, True)
            for e in range(E - 3, E):
                body(e, e % 2, e // 2, e < E - 1)

        def load_expert(sp, e, odd):
            sp.dma_start(raw_e[odd], eW[e].rearrange("(o p) h -> p o h", p=P)).then_inc(e_loaded[odd], 16)

        def ffn_sync(sp):
            sp.wait_ge(chunk_out, ALL_CHUNKS)
            sp.wait_ge(x2_stored, 16 * B)
            sp.wait_ge(y_zeroed, 1)
            sp.dma_start(g_raw, gW).then_inc(g_loaded, 16)
            sp.dma_start(e_bias, eb).then_inc(g_loaded, 16)
            for t in range(TT):
                n = min(P, T - t * P)
                sp.dma_start(y[0:n, t], x2_dram.rearrange("b l d -> (b l) d")[t * P:t * P + n]).then_inc(y_loaded[t], 16)
                if t == 3:
                    load_expert(sp, 0, 0)
            load_expert(sp, 1, 1)

            def next_raw(e, odd, pair, more):
                if not isinstance(e, int) or e < E - 2:
                    wait_alone(sp, e_low, KD * (e + 1))
                    load_expert(sp, e + 2, odd)
            experts(sp, next_raw)
            for t in range(TT):
                n = min(P, T - t * P)
                sp.wait_ge(y_done, TT * (E - 1) + t + 1)
                sp.dma_start(out.rearrange("b l d -> (b l) d")[t * P:t * P + n], y[0:n, t]).then_inc(y_stored, 16)
            sp.wait_ge(y_stored, 16 * TT)

        def pe_expert_T(pe, e, odd, pair, k):
            c = KD * e + k
            if k == 0:
                pe.wait_ge(e_loaded[odd], 16 * (pair + 1))
            if not (isinstance(c, int) and c < 2):
                pe.wait_ge(e_low, c - 1)
            for o in range(KD):
                last = pe.transpose(psum[:, 4 + k % 2, o * P:(o + 1) * P], raw_e[odd][:, o, k * P:(k + 1) * P], ident[:])
            last.then_inc(e_T, 1)

        def ffn_tensor(pe):
            pe.wait_ge(chunk_out, ALL_CHUNKS)
            pe.wait_ge(g_loaded, 32)
            for k in range(KD):
                last = pe.transpose(psum[:, 7, k * E:(k + 1) * E], g_raw[:, k * P:(k + 1) * P], ident[0:E, 0:E])
            last.then_inc(gT_ready, 1)
            pe.wait_ge(gT_low, 1)
            for t in range(TT):
                pe.wait_ge(f_norm, t + 1)
                if t >= 4:
                    pe.wait_ge(f_low, t - 3)
                for k in range(KD):
                    last = pe.transpose(psum[:, t % 4, k * P:(k + 1) * P], y_norm[t % 2][:, k * P:(k + 1) * P], ident[:])
                last.then_inc(f_T, 1)
                if t >= 1:
                    pe_logits(pe, t - 1)
            pe_logits(pe, TT - 1).then_inc(logits_ready, 1)
            for k in range(KD):
                pe_expert_T(pe, 0, 0, 0, k)
            pe.wait_ge(route, ROUTED)
            for t in range(TT):
                if t >= 4 and t % 4 == 0:
                    pe.wait_ge(tokT_out, t // 4)
                last = pe.transpose(psum[0:E, 6, (t % 4) * P:(t % 4 + 1) * P], gates[:, t], ident[:])
                if t % 4 == 3 or t == TT - 1:
                    last.then_inc(tokT_ready, 1)
            for t in range(TT):
                pe.wait_ge(tokT_out, t // 4 + 1)
                if t >= 2:
                    pe.wait_ge(eb_out, t - 1)
                pe.matmul(psum[:, 2 + t % 2, 0:D], gT_tok[:, t], e_bias, start=True, stop=True).then_inc(eb_ready, 1)

            def expert(e, odd, pair, more):
                for t in range(TT):
                    c = TT * e + t
                    if t == 0:
                        pe.wait_ge(e_low, KD * (e + 1))
                    if not (isinstance(e, int) and c < 2):
                        pe.wait_ge(y_done, c - 1)
                    split3(pe, psum[:, (t + odd) % 4, 0:D],
                           [(lambda p, k=k: xT3[:, p, k, t * P:(t + 1) * P], lambda p, k=k: wT_e[odd][:, k, p])
                            for k in range(KD)]).then_inc(y_ready, 1)
                    if more and t % 3 == 1 and t // 3 < KD:
                        pe_expert_T(pe, e + 1, 1 - odd, pair + odd, t // 3)
            pe.wait_ge(eb_out, TT)
            experts(pe, expert)

        def pe_logits(pe, t):
            pe.wait_ge(f_low, t + 1)
            return split3(pe, psum[:, 7, 64 + t * E:64 + (t + 1) * E],
                          [(lambda p, k=k: xT3[:, p, k, t * P:(t + 1) * P], lambda p, k=k: g_T[:, p, k])
                           for k in range(KD)])

        def ffn_scalar(act):
            act.wait_ge(gT_ready, 1)
            act.activation(g_T[:, 0].rearrange("p k e -> p (k e)"), psum[:, 7, 0:KD * E], ACT.Copy, scale=WSCALE)\
               .then_inc(gT_high, 1)
            for t in range(TT):
                act.wait_ge(f_T, t + 1)
                act.activation(xT3[:, 0, :, t * P:(t + 1) * P], psum[:, t % 4].rearrange("p (k t) -> p k t", k=KD),
                               ACT.Copy).then_inc(f_high, 1)

            def expert_high(e, odd, k):
                act.wait_ge(e_T, KD * e + k + 1)
                act.activation(wT_e[odd][:, k, 0], psum[:, 4 + k % 2], ACT.Copy, scale=WSCALE).then_inc(e_high, 1)
            for k in range(KD):
                expert_high(0, 0, k)
            act.wait_ge(route, 3)
            act.activation(gates, gates, ACT.Exp).then_inc(g_exp, 1)
            for i in range((TT + 3) // 4):
                act.wait_ge(tokT_ready, i + 1)
                n = min(4, TT - 4 * i)
                act.activation(gT_tok[:, 4 * i:4 * i + n].rearrange("e t p -> e (t p)"), psum[0:E, 6, 0:n * P],
                               ACT.Copy).then_inc(tokT_out, 1)
            experts(act, lambda e, odd, pair, more: [expert_high(e + 1, 1 - odd, k) for k in range(KD)] if more else None)

        def ffn_vector(dve):
            dve.wait_ge(chunk_out, ALL_CHUNKS)
            dve.memset(y[TLAST:P, TT - 1], 0.0).then_inc(y_zeroed, 1)
            dve.wait_ge(gT_high, 1)
            dve.scalar_tensor_tensor(g_T[:, 1].rearrange("p k e -> p (k e)"), psum[:, 7, 0:KD * E], WSCALE,
                                     g_T[:, 0].rearrange("p k e -> p (k e)"), ALU.mult, ALU.subtract)\
               .then_inc(gT_low, 1)
            for t in range(TT):
                dve.wait_ge(y_loaded[t], 16)
                if t >= 2:
                    dve.wait_ge(f_stats, t - 1)
                dve.bn_stats(stats3[:, t % 2], y[:, t]).then_inc(f_bn, 1)
                dve.wait_ge(f_bn, t + 1)
                dve.bn_aggr(moments3[:, t], stats3[:, t % 2]).then_inc(f_stats, 1)

            def low(t):
                dve.wait_ge(f_high, t + 1)
                dve.tensor_tensor(xT3[:, 1, :, t * P:(t + 1) * P], psum[:, t % 4].rearrange("p (k t) -> p k t", k=KD),
                                  xT3[:, 0, :, t * P:(t + 1) * P], ALU.subtract).then_inc(f_low, 1)
            dve.wait_ge(f_rstd, 1)
            for t in range(TT):
                if t >= 2:
                    dve.wait_ge(f_T, t - 1)
                dve.tensor_scalar(y_norm[t % 2], y[:, t], nmean3[:, t:t + 1], rstd3[:, t:t + 1], ALU.add, ALU.mult)\
                   .then_inc(f_norm, 1)
                if t >= 1:
                    low(t - 1)
            low(TT - 1)

            def expert_low(e, odd, k):
                dve.wait_ge(e_high, KD * e + k + 1)
                dve.scalar_tensor_tensor(wT_e[odd][:, k, 1], psum[:, 4 + k % 2], WSCALE, wT_e[odd][:, k, 0],
                                         ALU.mult, ALU.subtract).then_inc(e_low, 1)
            done = [0]

            def step(op):
                op.then_inc(route, 1)
                done[0] += 1
                dve.wait_ge(route, done[0])

            def over(a):
                return a[:].unsqueeze(2).to_broadcast([P, TT, E])
            dve.wait_ge(logits_ready, 1)
            step(dve.scalar_tensor_tensor(gates, psum[:, 7, 64:64 + TT * E].rearrange("p (t e) -> p t e", e=E),
                                          1.0 / WSCALE, g_bias[:].unsqueeze(1).to_broadcast([P, TT, E]),
                                          ALU.mult, ALU.add))
            step(dve.tensor_reduce(best[:], gates, AXIS.X, ALU.max))
            step(dve.tensor_tensor(gates, gates, over(best), ALU.subtract))
            for k in range(KD):
                expert_low(0, 0, k)
            dve.wait_ge(g_exp, 1)
            step(dve.tensor_reduce(best[:], gates, AXIS.X, ALU.add))
            step(dve.reciprocal(best[:], best[:]))
            step(dve.tensor_tensor(gates, gates, over(best), ALU.mult))
            dve.wait_ge(rank_set, E)
            for i in range(2):
                src = gates if i == 0 else tie
                step(dve.tensor_reduce(best[:], src, AXIS.X, ALU.max))
                step(dve.tensor_tensor(first, src, over(best), ALU.is_ge))
                step(dve.tensor_tensor(first, first, rank[:].unsqueeze(1).to_broadcast([P, TT, E]), ALU.mult))
                step(dve.tensor_reduce(best[:], first, AXIS.X, ALU.max))
                if i == 0:
                    step(dve.tensor_tensor(picked, first, over(best), ALU.is_equal))
                    step(dve.scalar_tensor_tensor(tie, picked, -4.0, gates, ALU.mult, ALU.add))
                else:
                    step(dve.tensor_tensor(first, first, over(best), ALU.is_equal))
                    step(dve.tensor_tensor(picked, picked, first, ALU.add))
            step(dve.tensor_tensor(gates, gates, picked, ALU.mult))
            step(dve.tensor_scalar(g_scaled, gates, 1.0 / WSCALE, None, ALU.mult))
            step(dve.tensor_copy(g_now[:, 0], g_scaled[:, :, 0]))
            assert done[0] == ROUTED
            for t in range(TT):
                dve.wait_ge(eb_ready, t + 1)
                dve.tensor_tensor(y[:, t], psum[:, 2 + t % 2, 0:D], y[:, t], ALU.add).then_inc(eb_out, 1)

            def expert(e, odd, pair, more):
                dve.wait_ge(y_done, TT * e) if not isinstance(e, int) or e > 0 else None
                dve.tensor_copy(g_now[:, odd], g_scaled[:, :, e]).then_inc(g_now_set, 1)
                dve.wait_ge(g_now_set, e + 1)
                for t in range(TT):
                    dve.wait_ge(y_ready, TT * e + t + 1)
                    dve.scalar_tensor_tensor(y[:, t], psum[:, (t + odd) % 4, 0:D], g_now[:, odd, t:t + 1], y[:, t],
                                             ALU.mult, ALU.add).then_inc(y_done, 1)
                    if more and t % 3 == 1 and t // 3 < KD:
                        expert_low(e + 1, 1 - odd, t // 3)
            dve.wait_ge(eb_out, TT)
            experts(dve, expert)

        def ffn_gpsimd(pool):
            pool.wait_ge(f_stats, TT)
            pool.tensor_scalar(nmean3[:], moments3[:, :, 0], -1.0, None, ALU.mult).then_inc(f_half, 1)
            pool.tensor_scalar(rstd3[:], moments3[:, :, 1], EPS, None, ALU.add).then_inc(f_half, 1)
            pool.wait_ge(f_half, 2)
            pool.tensor_tensor(rstd3[:], rstd3[:], half[:].to_broadcast([P, TT]), ALU.pow).then_inc(f_rstd, 1)


        def pipeline(engine, body):
            peel_from = B - 3
            body(Iteration(-1, True, cross=False, tail=False))
            body(Iteration(0, False, tail=False))
            with engine.Fori(0, (peel_from - 1) // 2) as i:
                body(Iteration(2 * i + 1, True))
                body(Iteration(2 * i + 2, False))
            for n in range(peel_from, B):
                body(Iteration(n, n % 2 == 1, prep=n < B - 1))
            body(Iteration(B, False, cross=False, prep=False))

        block = stack.enter_context(nc.Block())

        def load_x(sp, m):
            sp.dma_start(x_in[:], x[m]).then_inc(x_loaded, 16)

        def load_ctx(sp, m):
            full = CT - 1
            sp.dma_start(c_raw[:, 0:full], ctx[m, 0:full * CW].rearrange("(t p) c -> p t c", p=CW))\
              .then_inc(ctx_loaded, 16)
            sp.dma_start(c_raw[0:LC - full * CW, full], ctx[m, full * CW:LC]).then_inc(ctx_loaded, 16)

        def sync_iteration(sp, it):
            n, m = it.n, it.n + 1
            if it.tail:
                wait_alone(sp, chunk_out, it.done("TP"))
                sp.dma_start(x2_dram[n - 1], x_mid[1 if not it.odd else 0][:]).then_inc(x2_stored, 16)
            if it.prep and not (isinstance(n, int) and n == B - 2):
                wait_alone(sp, chunk_out, it.done("SO1"))
                load_ctx(sp, n + 2)
            if it.prep:
                odd_m = not it.odd
                if not (isinstance(n, int) and n == B - 2):
                    wait_alone(sp, chunk_out, it.done("OP"))
                    load_x(sp, n + 2)
                if it.tail:
                    wait_alone(sp, score_ready, H * n)
                wait_alone(sp, chunk_out, it.done(f"CK{2 * KD - 1}"))
                for c in range(HT):
                    for r, part in enumerate((0, 0, 1)):
                        sp.dma_start(stack_k[odd_m][DH * r:DH * (r + 1), c::HT],
                                     split_k[DH * c:DH * (c + 1), part]).then_inc(k_stacked[c], 16)
                wait_alone(sp, cq_split, m + 1)
                for c in range(HT):
                    for r, slot in enumerate((QHIGH, QLOW, QHIGH)):
                        sp.dma_start(stack_q[odd_m][DH * r:DH * (r + 1), c::HT],
                                     split_qk[DH * c:DH * (c + 1), slot]).then_inc(cq_stacked[c], 16)

        @block.sync
        def _(sp):
            sp.dma_start(rope_t[:], rope).then_inc(const_loaded, 16)
            for i, b in enumerate((sbq, sbk, cbq, cbkv[0:D], sbv, cbkv[D:2 * D])):
                sp.dma_start(b_rows[KD * i:KD * (i + 1)], b.rearrange("(m p) -> m p", p=P)).then_inc(const_loaded, 16)
            for dst, b in ((b_so, sbo), (b_cp, cbp)):
                sp.dma_start(dst[:], b.partition_broadcast(L)).then_inc(const_loaded, 16)
            sp.dma_start(g_bias[:], gb.partition_broadcast(P)).then_inc(const_loaded, 16)
            raw = flat32[:, 0:5 * KD * D].rearrange("p (w k f) -> p w k f", w=5, k=KD)
            sp.dma_start(raw[:, 0], sWq.rearrange("(k p) f -> p k f", p=P)).then_inc(raw_loaded[0], 16)
            sp.dma_start(raw[:, 1], sWk.rearrange("(k p) f -> p k f", p=P)).then_inc(raw_loaded[1], 16)
            load_x(sp, 0)
            sp.wait_ge(setup_done, 2)
            load_ctx(sp, 0)
            sp.dma_start(raw[:, 2], sWv.rearrange("(k p) f -> p k f", p=P)).then_inc(raw_loaded[2], 16)
            sp.dma_start(raw[:, 3], sWo.rearrange("(k p) f -> p k f", p=P)).then_inc(raw_loaded[3], 16)
            sp.dma_start(raw[:, 4], cWq.rearrange("(k p) f -> p k f", p=P)).then_inc(raw_loaded[4], 16)
            sp.wait_ge(wT_low, 8)
            sp.dma_start(raw[:, 0], cWp.rearrange("(k p) f -> p k f", p=P)).then_inc(raw2_loaded, 16)
            sp.wait_ge(wT_low, 16)
            sp.dma_start(flat32[:, KD * D:KD * D + KC * 2 * D].rearrange("p (k f) -> p k f", k=KC),
                         cWkv.rearrange("(k p) f -> p k f", p=P)).then_inc(raw2_loaded, 16)
            sp.wait_ge(w_low, 3)
            pipeline(sp, lambda it: sync_iteration(sp, it))
            ffn_sync(sp)

        def pe_chunk(pe, it, name):
            m = it.n + 1
            odd_m = not it.odd
            f = filler[it.bank(name)]
            done = it.done(name)
            if not (isinstance(done, int) and done <= 2):
                pe.wait_ge(chunk_out, done - 2)
            last = None
            kind, i = name[:2], int(name[2:]) if name[2:].isdigit() else 0
            if name in ("X1T", "X2T"):
                pe.wait_ge(norm_done, 2 * m + (1 if name == "X1T" else 2))
                for k in range(KD):
                    last = pe.transpose(f[:, k * L:(k + 1) * L], x_norm[:, k * P:(k + 1) * P], ident[0:L, 0:L])
            elif name in ("SQ", "SK", "CQ"):
                pe.wait_ge(chunk_out, it.done("X2T" if name == "CQ" else "X1T"))
                w = w_cross["q"] if name == "CQ" else w_self[name[1].lower()]
                for o in range(KD):
                    last = split3(pe, f[:, o * L:(o + 1) * L],
                                  [(lambda p, k=k: w[:, k, p, o * P:(o + 1) * P], lambda p, k=k: xT[:, p, k])
                                   for k in range(KD)])
            elif name == "SV":
                last = split3(pe, f[0:L, 0:D], [(lambda p, k=k: xT[:, p, k], lambda p, k=k: w_self["v"][:, k, p])
                                                for k in range(KD)])
            elif kind == "SS":
                pe.wait_ge(qk_split, 2 * m + 2)
                rows = slice(DH * i, DH * (i + 1))
                for o in range(KD):
                    for c, (a, b) in enumerate(((QHIGH, KHIGH), (QHIGH, KLOW), (QLOW, KHIGH))):
                        last = pe.matmul(f[0:L, o * L:(o + 1) * L], split_qk[rows, a, o], split_qk[rows, b, o],
                                         start=c == 0, stop=c == 2)
            elif kind == "SP":
                pe.wait_ge(s_exp, 2 * m + i // 2 + 1)
                for j in range(4):
                    last = pe.transpose(f[0:L, j * L:(j + 1) * L], s_sc[:, i, j * L:(j + 1) * L], ident[0:L, 0:L])
            elif kind == "SO":
                pe.wait_ge(chunk_out, it.done("SP3"))
                for j in range(H // 2):
                    h = H // 2 * i + j
                    for p in range(2):
                        c = (p * 4 + h // 4) * L
                        last = pe.matmul(f[0:L, j * 2 * DH:(j + 1) * 2 * DH], s_scT[:, h % 4, c:c + L],
                                         sv[:, h].rearrange("k p d -> k (p d)"), start=p == 0, stop=p == 1)
            elif name in ("OT", "TT"):
                if name == "OT":
                    pe.wait_ge(s_out_done, 2 * m + 2)
                else:
                    pe.wait_ge(c_out_done, it.n)
                src = s_out if name == "OT" else c_out
                for k in range(KD):
                    last = pe.transpose(f[:, k * L:(k + 1) * L], src[:, k * P:(k + 1) * P], ident[0:L, 0:L])
            elif name in ("OP", "TP"):
                pe.wait_ge(chunk_out, it.done("OT" if name == "OP" else "TT"))
                w = w_self["o"] if name == "OP" else w_cross["p"]
                last = split3(pe, f[0:L, 0:D], [(lambda p, k=k: oT[:, p, k], lambda p, k=k: w[:, k, p])
                                                for k in range(KD)])
            elif kind == "CX":
                pe.wait_ge(ctx_loaded, 16 * 2 * (m + 1))
                k, hf = i // 2, i % 2
                for j in range(3):
                    last = pe.transpose(f[:, j * CW:(j + 1) * CW], c_raw[:, 3 * hf + j, k * P:(k + 1) * P],
                                        ident[0:CW, 0:CW])
            elif kind == "CK":
                pe.wait_ge(chunk_out, it.done("CX5"))
                o, hf = i // 2, i % 2
                last = split3(pe, f[:, 0:HC],
                              [(lambda p, k=k: w_kv[:, k, p, o * P:(o + 1) * P],
                                lambda p, k=k: cT[:, k, p, hf * HC:(hf + 1) * HC]) for k in range(KC)])
            elif kind == "CV":
                pe.wait_ge(chunk_out, it.done("CX5"))
                last = split3(pe, f[0:CW, 0:D],
                              [(lambda p, k=k: cT[:, k, p, i * CW:(i + 1) * CW],
                                lambda p, k=k: w_kv[:, k, p, D:2 * D]) for k in range(KC)])
            last.then_inc(chunk_ready, 1)

        def pe_scores(pe, n, odd, h):
            g = H * n + h
            if not (isinstance(g, int) and g < 2):
                pe.wait_ge(exp_done, g - 1)
            if h < HT:
                pe.wait_ge(k_stacked[h], 16 * 3 * (n + 1))
                pe.wait_ge(cq_stacked[h], 16 * 3 * (n + 1))
            for hf in range(2):
                last = pe.matmul(score[h % 2][0:L, hf, 0:HC], stack_q[odd][:, h],
                                 stack_k[odd][:, h, hf * HC:(hf + 1) * HC], start=True, stop=True)
            last.then_inc(score_ready, 1)

        def pe_head_out(pe, n, odd, h):
            pe.wait_ge(pT_out, H * n + h + 1)
            o = OCOL + 2 * DH * (h % 2)
            for t in range(CT):
                for p in range(2):
                    last = pe.matmul(pT[0:L, h % 4 // 2, o:o + 2 * DH], probT[:, p, t * L:(t + 1) * L],
                                     cv[odd][:, t, h].rearrange("k p d -> k (p d)"),
                                     start=t + p == 0, stop=t + p == CT)
            last.then_inc(head_done, 1)

        def pe_transpose_probs(pe, n, h):
            g = H * n + h
            pe.wait_ge(exp_done, g + 1)
            if not (isinstance(g, int) and g < 1):
                pe.wait_ge(pT_out, g)
            for t in range(CT):
                last = pe.transpose(pT[0:CW, t // 3, (t % 3) * L:(t % 3 + 1) * L],
                                    prob[h % 2][:, t * CW:(t + 1) * CW], ident[0:L, 0:L])
            last.then_inc(pT_ready, 1)

        def pe_iteration(pe, it):
            n = it.n
            begun = not (isinstance(n, int) and n <= 0)
            for h in range(H):
                for what in PE_ORDER:
                    if what == "S":
                        if it.cross and h + 1 < H:
                            pe_scores(pe, n, it.odd, h + 1)
                        elif h + 1 == H and it.prep:
                            pe_scores(pe, n + 1, not it.odd, 0)
                    elif what == "O":
                        if h == 0 and begun:
                            pe_head_out(pe, n - 1, not it.odd, H - 1)
                        elif h > 0 and it.cross:
                            pe_head_out(pe, n, it.odd, h - 1)
                    elif what == "T":
                        if it.cross:
                            pe_transpose_probs(pe, n, h)
                    else:
                        for name in it.steps[h][int(what):][:1]:
                            pe_chunk(pe, it, name)

        @block.tensor
        def _(pe):
            pe.wait_ge(ident_done, 2)
            pe.wait_ge(const_loaded, 16 * 10)
            pe.transpose(psum[:, 7, 0:6 * KD], b_rows[:], ident[0:6 * KD, 0:6 * KD]).then_inc(bias_ready_T, 1)
            raw = flat32[:, 0:5 * KD * D].rearrange("p (w k f) -> p w k f", w=5, k=KD)
            for i in range(4 * KD):
                w, k = i // KD, i % KD
                pe.wait_ge(raw_loaded[w], 16)
                if i == 7:
                    pe.wait_ge(bias_done, 1)
                if i >= 8:
                    pe.wait_ge(wT_low, i - 7)
                for o in range(KD):
                    last = pe.transpose(psum[:, i % 8, o * P:(o + 1) * P], raw[:, w, o, k * P:(k + 1) * P], ident[:])
                last.then_inc(wT_ready, 1)
            pe.wait_ge(wT_low, 4 * KD)
            pe.wait_ge(w_low, 3)
            pe.wait_ge(setup_done, 3)
            pe.wait_ge(bv_split, 1)
            for i, w in enumerate((w_self["o"], w_cross["p"])):
                split3(pe, psum[0:L, 6 + i, 0:D],
                       [(lambda p, k=k: b_value[:, i, p, k:k + 1].to_broadcast([P, L]), lambda p, k=k: w[:, k, p])
                        for k in range(KD)]).then_inc(bv_ready, 1)
            pe.wait_ge(bv_folded, 2)
            pipeline(pe, lambda it: pe_iteration(pe, it))
            ffn_tensor(pe)

        def act_chunk(act, it, name):
            if name not in SPLIT:
                return
            f = filler[it.bank(name)]
            act.wait_ge(chunk_ready, it.done(name))
            kind, i = name[:2], int(name[2:]) if name[2:].isdigit() else 0
            if name in ("X1T", "X2T", "OT", "TT"):
                dst = (xT if name[0] == "X" else oT)[:, 0].rearrange("p k l -> p (k l)")
                op = act.activation(dst, f[:, 0:KD * L], ACT.Copy)
            elif name == "SV":
                op = act.activation(sv[:, :, 0], f[0:L, 0:D].rearrange("k (h d) -> k h d", h=H), ACT.Copy)
            elif kind == "SP":
                if i % 2 == 0:
                    act.wait_ge(s_sum_done, 2 * (it.n + 1) + i // 2 + 1)
                op = act.activation(s_scT[:, i, 0:4 * L], f[0:L, 0:4 * L], ACT.Copy)
            elif kind == "CX":
                op = act.activation(cT[:, i // 2, 0, (i % 2) * HP:(i % 2 + 1) * HP], f[:, 0:HP], ACT.Copy)
            elif kind == "CK":
                if i == 0 and not (isinstance(it.n, int) and it.n < 0):
                    for c in range(HT):
                        act.wait_ge(k_stacked[c], 16 * 3 * (it.n + 1))
                op = act.activation(split_k[:, 0, i // 2, (i % 2) * HC:(i % 2 + 1) * HC], f[:, 0:HC],
                                    ACT.Identity, bias=b_part[:, 3, i // 2:i // 2 + 1])
            elif kind == "CV":
                op = act.activation(cv[not it.odd][:, i, :, 0], f[0:CW, 0:D].rearrange("k (h d) -> k h d", h=H), ACT.Copy)
            op.then_inc(chunk_high, 1)

        def act_exp(act, n, odd, h):
            act.wait_ge(bias_ready, H * n + h + 1)
            act.activation(prob[h % 2][:, 0:LC].rearrange("q (a k) -> q a k", a=2), score[h % 2][0:L, :, 0:HC],
                           ACT.Exp, bias=c_bias[:, int(odd), h:h + 1], scale=SOFT,
                           accum_out=c_sum[:, int(odd), h:h + 1]).then_inc(exp_done, 1)

        def act_probs_high(act, n, h):
            act.wait_ge(pT_ready, H * n + h + 1)
            act.activation(probT[:, 0].rearrange("k (a c) -> k a c", a=2), pT[0:CW, :, 0:3 * L], ACT.Copy)\
               .then_inc(pT_high, 1)

        def act_iteration(act, it):
            n = it.n
            for h in range(H):
                for what in ACT_ORDER:
                    if what == "E":
                        if it.cross and h + 1 < H:
                            act_exp(act, n, it.odd, h + 1)
                        elif h + 1 == H and it.prep:
                            act_exp(act, n + 1, not it.odd, 0)
                    elif what == "P":
                        if it.cross:
                            act_probs_high(act, n, h)
                    else:
                        for name in it.steps[h][int(what):][:1]:
                            act_chunk(act, it, name)
                if h in EXP_STEPS and it.prep:
                    i = EXP_STEPS.index(h)
                    act.wait_ge(s_shifted, 4 * (n + 1) + 2 * i + 2)
                    act.activation(s_sc[:, 2 * i:2 * i + 2], s_sc[:, 2 * i:2 * i + 2], ACT.Exp, scale=SOFT)\
                       .then_inc(s_exp, 1)

        @block.scalar
        def _(act):
            raw = flat32[:, 0:5 * KD * D].rearrange("p (w k f) -> p w k f", w=5, k=KD)
            for i in range(4 * KD):
                act.wait_ge(wT_ready, i + 1)
                act.activation(w_self["qkvo"[i // KD]][:, i % KD, 0], psum[:, i % 8], ACT.Copy, scale=WSCALE)\
                   .then_inc(wT_high, 1)
            act.wait_ge(raw_loaded[4], 16)
            act.activation(w_cross["q"][:, :, 0], raw[:, 4], ACT.Copy, scale=WSCALE).then_inc(w_high, 1)
            act.wait_ge(raw2_loaded, 16 * 2)
            act.activation(w_cross["p"][:, :, 0], raw[:, 0], ACT.Copy, scale=WSCALE).then_inc(w_high, 1)
            kv = flat32[:, KD * D:KD * D + KC * 2 * D].rearrange("p (k f) -> p k f", k=KC)
            act.activation(w_kv[:, :, 0], kv, ACT.Copy, scale=WSCALE).then_inc(w_high, 1)
            act.wait_ge(bias_done, 1)
            pipeline(act, lambda it: act_iteration(act, it))
            ffn_scalar(act)

        def dve_chunk(dve, it, name):
            n, m = it.n, it.n + 1
            odd_m = not it.odd
            f = filler[it.bank(name)]
            kind, i = name[:2], int(name[2:]) if name[2:].isdigit() else 0
            if name in SPLIT:
                dve.wait_ge(chunk_high, it.high_done(name))
            else:
                dve.wait_ge(chunk_ready, it.done(name))

            def low(dst, src, high):
                return dve.tensor_tensor(dst, src, high, ALU.subtract)

            if name in ("X1T", "X2T", "OT", "TT"):
                d = xT if name[0] == "X" else oT
                op = low(d[:, 1].rearrange("p k l -> p (k l)"), f[:, 0:KD * L], d[:, 0].rearrange("p k l -> p (k l)"))
            elif name in ("SQ", "SK"):
                if not (isinstance(n, int) and n < 0):
                    dve.wait_ge(cq_split, m) if name == "SQ" else dve.wait_ge(qk_split, 2 * m)
                op = dve.tensor_tensor((tmp_q if name == "SQ" else tmp_k)[:],
                                       f[:, 0:KD * L].rearrange("p (k l) -> p k l", k=KD),
                                       b_part[:, int(name == "SK")].unsqueeze(2).to_broadcast([P, KD, L]), ALU.add)
            elif name == "CQ":
                dve.wait_ge(qk_split, 2 * m + 1)
                op = dve.tensor_tensor(tmp_q[:], f[:, 0:KD * L].rearrange("p (k l) -> p k l", k=KD),
                                       b_part[:, 2].unsqueeze(2).to_broadcast([P, KD, L]), ALU.add)
            elif name == "SV":
                op = low(sv[:, :, 1], f[0:L, 0:D].rearrange("k (h d) -> k h d", h=H), sv[:, :, 0])
            elif kind == "SS":
                op = dve.tensor_tensor(s_sc[:, i].rearrange("q (j k) -> q j k", j=4),
                                       f[0:L, 0:4 * L].rearrange("q (j k) -> q j k", j=4),
                                       mask[:].unsqueeze(1).to_broadcast([L, 4, L]), ALU.add)
            elif kind == "SP":
                op = low(s_scT[:, i, 4 * L:8 * L], f[0:L, 0:4 * L], s_scT[:, i, 0:4 * L])
            elif kind == "SO":
                parts = f[0:L].rearrange("q (h p d) -> q h p d", p=2, d=DH)
                op = dve.tensor_reduce(s_out[:, i * D // 2:(i + 1) * D // 2].rearrange("q (h d) -> q h d", h=H // 2),
                                       parts.rearrange("q h p d -> q h d p"), AXIS.X, ALU.add)
            elif name == "OP":
                dve.wait_ge(x_biased, 2 * m + 1)
                if not (isinstance(n, int) and n < 1):
                    dve.wait_ge(x2_stored, 16 * n)
                op = dve.scalar_tensor_tensor(x_mid[odd_m][:], f[0:L, 0:D], PSCALE, x_in[:], ALU.mult, ALU.add)
            elif name == "TP":
                buf = x_mid[not it.odd]
                dve.wait_ge(x_biased, 2 * n)
                op = dve.scalar_tensor_tensor(buf[:], f[0:L, 0:D], PSCALE, buf[:], ALU.mult, ALU.add)
            elif kind == "CX":
                c = slice((i % 2) * HP, (i % 2 + 1) * HP)
                op = low(cT[:, i // 2, 1, c], f[:, 0:HP], cT[:, i // 2, 0, c])
            elif kind == "CK":
                c = slice((i % 2) * HC, (i % 2 + 1) * HC)
                op = dve.scalar_tensor_tensor(split_k[:, 1, i // 2, c], f[:, 0:HC], b_part[:, 3, i // 2:i // 2 + 1],
                                              split_k[:, 0, i // 2, c], ALU.add, ALU.subtract)
            elif kind == "CV":
                op = low(cv[odd_m][:, i, :, 1], f[0:CW, 0:D].rearrange("k (h d) -> k h d", h=H), cv[odd_m][:, i, :, 0])
            op.then_inc(chunk_out, 1)

        def dve_max(dve, n, odd, h):
            g = H * n + h
            dve.wait_ge(score_ready, g + 1)
            if not (isinstance(g, int) and g < 2 * H):
                dve.wait_ge(exp_done, g - H)
            dve.tensor_reduce(c_max[:, int(odd), h:h + 1], score[h % 2][0:L, :, 0:HC], AXIS.XY, ALU.max)\
               .then_inc(max_done, 1)
            dve.wait_ge(max_done, g + 1)
            dve.tensor_scalar(c_bias[:, int(odd), h:h + 1], c_max[:, int(odd), h:h + 1], -SOFT, None, ALU.mult)\
               .then_inc(bias_ready, 1)

        def dve_probs_low(dve, n, h):
            dve.wait_ge(pT_high, H * n + h + 1)
            return dve.tensor_tensor(probT[:, 1].rearrange("k (a c) -> k a c", a=2), pT[0:CW, :, 0:3 * L],
                                     probT[:, 0].rearrange("k (a c) -> k a c", a=2), ALU.subtract)

        def dve_inverse(dve, n, odd):
            dve.wait_ge(exp_done, H * n + H)
            if not (isinstance(n, int) and n < 1):
                dve.wait_ge(c_out_done, n)
            dve.reciprocal(c_rinv[:], c_sum[:, int(odd)]).then_inc(c_rinv_done, 1)

        def dve_heads_sum(dve, n, group):
            dve.wait_ge(head_done, H * n + 4 * group + 4)
            parts = pT[0:L, :, OCOL:OCOL + 4 * DH].rearrange("q a (b p d) -> q a b p d", p=2, d=DH)
            return dve.tensor_reduce(
                c_out[:, 4 * DH * group:4 * DH * (group + 1)].rearrange("q (a b d) -> q a b d", a=2, b=2),
                parts.rearrange("q a b p d -> q a b d p"), AXIS.X, ALU.add)

        def dve_stats(dve, src, count):
            if not (isinstance(count, int) and count < 1):
                dve.wait_ge(ln_shift, 2 * count)
            dve.bn_stats(stats[0:L], src).then_inc(bn_done, 1)
            wait_alone(dve, bn_done, count + 1)
            dve.bn_aggr(moments[0:L], stats[0:L]).then_inc(stats_done, 1)

        def dve_iteration(dve, it):
            n, m = it.n, it.n + 1
            begun = not (isinstance(n, int) and n <= 0)
            for h in range(H):
                if h in SUM_STEPS and it.prep:
                    i = SUM_STEPS.index(h)
                    dve.wait_ge(s_exp, 2 * m + i + 1)
                    dve.tensor_reduce(s_sum[:, 8 * i:8 * i + 8],
                                      s_sc[:, 2 * i:2 * i + 2].rearrange("q g (j k) -> q (g j) k", j=4),
                                      AXIS.X, ALU.add).then_inc(s_sum_done, 1)
                    if i == 1:
                        dve.wait_ge(s_sum_done, 2 * m + 2)
                        dve.reciprocal(s_rinv[:].rearrange("q (o g) -> q g o", g=HT),
                                       s_sum[:].rearrange("q (g o) -> q g o", g=HT)).then_inc(s_rinv_done, 1)
                for what in DVE_ORDER:
                    if what == "M":
                        if it.cross and h + 1 < H:
                            dve_max(dve, n, it.odd, h + 1)
                        elif h + 1 == H and it.prep:
                            dve_max(dve, n + 1, not it.odd, 0)
                    elif what == "L":
                        dve_head(dve, it, h, begun)
                    else:
                        for name in it.steps[h][int(what):][:1]:
                            dve_prep(dve, it, name)
                if h == H - 2 and it.prep and not (isinstance(n, int) and n == B - 2):
                    dve.wait_ge(x_loaded, 16 * (n + 3))
                    dve_stats(dve, x_in[:], 2 * m + 2)

        def dve_head(dve, it, h, begun):
            n = it.n
            if it.cross:
                if h % 4 == 0 and (h > 0 or begun):
                    dve_probs_low(dve, n, h).then_inc(pT_low, 1)
                    dve_heads_sum(dve, n - (h == 0), (h // 4 + 3) % 4).then_inc(pT_out, 1)
                else:
                    dve_probs_low(dve, n, h).then_inc(pT_out, 1)
            elif h == 0 and begun:
                dve_heads_sum(dve, n - 1, 3).then_inc(c_summed, 1)
            if h == 0 and begun:
                dve_inverse(dve, n - 1, not it.odd)

        def dve_prep(dve, it, name):
            dve_chunk(dve, it, name)
            if name[:2] == "SS":
                i = int(name[2])
                dve.wait_ge(chunk_out, it.done(name))
                dve.tensor_reduce(s_max[:, 4 * i:4 * i + 4], s_sc[:, i].rearrange("q (j k) -> q j k", j=4),
                                  AXIS.X, ALU.max).then_inc(s_max_done, 1)
            if name == "OP":
                dve.wait_ge(chunk_out, it.done("OP"))
                dve_stats(dve, x_mid[not it.odd][:], 2 * (it.n + 1) + 1)

        @block.vector
        def _(dve):
            raw = flat32[:, 0:5 * KD * D].rearrange("p (w k f) -> p w k f", w=5, k=KD)
            dve.memset(ident[:], 0.0).then_inc(ident_done, 1)
            dve.memset(mask[:], 0.0).then_inc(setup_done, 1)
            dve.memset(c_raw[96:CW, CT - 1], 0.0).then_inc(setup_done, 1)
            for i in range(2):
                last = dve.memset(prob[i][:, LC:LCP], 0.0)
            last.then_inc(setup_done, 1)
            dve.memset(half[:], -0.5).then_inc(setup_done, 1)
            for e in range(E):
                dve.memset(rank[:, e:e + 1], float(E - e)).then_inc(rank_set, 1)
            dve.wait_ge(bias_ready_T, 1)
            dve.tensor_scalar(b_part[:].rearrange("p b k -> p (b k)"), psum[:, 7, 0:6 * KD], WSCALE, None, ALU.mult)\
               .then_inc(bias_done, 1)
            dve.wait_ge(bias_done, 1)
            dve.tensor_copy(b_value[:, :, 0], b_part[:, 4:6]).then_inc(bv_high, 1)
            dve.wait_ge(bv_high, 1)
            dve.tensor_tensor(b_value[:, :, 1], b_part[:, 4:6], b_value[:, :, 0], ALU.subtract).then_inc(bv_split, 1)
            dve.wait_ge(x_loaded, 16)
            dve_stats(dve, x_in[:], 0)
            for i in range(4 * KD):
                dve.wait_ge(wT_high, i + 1)
                w = w_self["qkvo"[i // KD]]
                dve.scalar_tensor_tensor(w[:, i % KD, 1], psum[:, i % 8], WSCALE, w[:, i % KD, 0],
                                         ALU.mult, ALU.subtract).then_inc(wT_low, 1)
            kv = flat32[:, KD * D:KD * D + KC * 2 * D].rearrange("p (k f) -> p k f", k=KC)
            for i, (w, src) in enumerate(((w_cross["q"], raw[:, 4]), (w_cross["p"], raw[:, 0]), (w_kv, kv))):
                dve.wait_ge(w_high, i + 1)
                dve.scalar_tensor_tensor(w[:, :, 1], src, WSCALE, w[:, :, 0], ALU.mult, ALU.subtract)\
                   .then_inc(w_low, 1)
            dve.wait_ge(setup_done, 5)
            for i, b in enumerate((b_so, b_cp)):
                dve.wait_ge(bv_ready, i + 1)
                dve.scalar_tensor_tensor(b[:], psum[0:L, 6 + i, 0:D], PSCALE, b[:], ALU.mult, ALU.add)\
                   .then_inc(bv_folded, 1)
            pipeline(dve, lambda it: dve_iteration(dve, it))
            ffn_vector(dve)

        def pool_norm(pool, src, count, x_bias):
            wait_alone(pool, stats_done, count + 1)
            pool.tensor_scalar(shift[0:L, 0:1], moments[0:L, 0:1], -1.0, None, ALU.mult).then_inc(ln_shift, 1)
            pool.tensor_scalar(shift[0:L, 1:2], moments[0:L, 1:2], EPS, None, ALU.add).then_inc(ln_shift, 1)
            pool.wait_ge(ln_shift, 2 * count + 2)
            pool.tensor_tensor(rstd[0:L], shift[0:L, 1:2], half[0:L], ALU.pow).then_inc(ln_rstd, 1)
            wait_alone(pool, ln_rstd, count + 1)
            pool.tensor_scalar(x_norm[:], src, shift[0:L, 0:1], rstd[0:L, 0:1], ALU.add, ALU.mult)\
                .then_inc(norm_done, 1)
            pool.wait_ge(norm_done, count + 1)
            pool.tensor_tensor(src, src, x_bias[:], ALU.add).then_inc(x_biased, 1)

        def pool_split_q(pool, count):
            pool.tensor_copy(split_qk[:, QHIGH], tmp_q[:]).then_inc(cq_high, 1)
            pool.wait_ge(cq_high, count + 1)
            return pool.tensor_tensor(split_qk[:, QLOW], tmp_q[:], split_qk[:, QHIGH], ALU.subtract)

        def pool_iteration(pool, it):
            n, m = it.n, it.n + 1
            begun = not (isinstance(n, int) and n <= 0)
            if it.prep:
                for i, name in enumerate(("SQ", "SK")):
                    tmp = (tmp_q, tmp_k)[i]
                    pool.wait_ge(chunk_out, it.done(name))
                    pool.tensor_tensor(tmp[:], tmp[:], rope_t[:].unsqueeze(1).to_broadcast([P, KD, L]), ALU.mult)\
                        .then_inc(qk_rotated, 1)
                    if i == 0 and not (isinstance(n, int) and n < 0):
                        for c in range(HT):
                            pool.wait_ge(cq_stacked[c], 16 * 3 * m)
                    wait_alone(pool, qk_rotated, 2 * m + i + 1)
                    if i == 0:
                        pool_split_q(pool, 2 * m).then_inc(qk_split, 1)
                    else:
                        pool.tensor_copy(split_qk[:, KHIGH], tmp_k[:]).then_inc(qk_high, 1)
                        pool.wait_ge(qk_high, m + 1)
                        pool.tensor_tensor(split_qk[:, KLOW], tmp_k[:], split_qk[:, KHIGH], ALU.subtract)\
                            .then_inc(qk_split, 1)
            if begun:
                pool.wait_ge(c_rinv_done, n)
                pool.wait_ge(pT_out, H * n + 1) if it.cross else pool.wait_ge(c_summed, 1)
                heads = c_out[:].rearrange("q (h d) -> q h d", h=H)
                pool.tensor_tensor(heads, heads, c_rinv[:].unsqueeze(2).to_broadcast([L, H, DH]), ALU.mult)\
                    .then_inc(c_out_done, 1)
            if it.prep:
                for g in range(4):
                    pool.wait_ge(s_max_done, 4 * m + g + 1)
                    scores = s_sc[:, g].rearrange("q (j k) -> q j k", j=4)
                    pool.tensor_tensor(scores, scores, s_max[:, 4 * g:4 * g + 4].unsqueeze(2).to_broadcast([L, 4, L]),
                                       ALU.subtract).then_inc(s_shifted, 1)
                for i in range(2):
                    pool.wait_ge(s_rinv_done, m + 1)
                    pool.wait_ge(chunk_out, it.done(f"SO{i}"))
                    heads = s_out[:, i * D // 2:(i + 1) * D // 2].rearrange("q (h d) -> q h d", h=H // 2)
                    pool.tensor_tensor(heads, heads, s_rinv[:, i * H // 2:(i + 1) * H // 2].unsqueeze(2)
                                       .to_broadcast([L, H // 2, DH]), ALU.mult).then_inc(s_out_done, 1)
                pool_norm(pool, x_mid[not it.odd][:], 2 * m + 1, b_cp)
                wait_alone(pool, chunk_out, it.done("CQ"))
                pool_split_q(pool, 2 * m + 1).then_inc(cq_split, 1)
                if not (isinstance(n, int) and n == B - 2):
                    pool_norm(pool, x_in[:], 2 * m + 2, b_so)

        @block.gpsimd
        def _(pool):
            pool.wait_ge(ident_done, 1)
            pool.affine_select(out=ident[:], in_=ident[:], compare_op=ALU.not_equal, fill=1.0, base=0,
                               pattern=[[-1, P]], channel_multiplier=1).then_inc(ident_done, 1)
            pool.wait_ge(setup_done, 4)
            pool.affine_select(out=mask[:], in_=mask[:], compare_op=ALU.is_ge, fill=MASKED, base=0,
                               pattern=[[-1, L]], channel_multiplier=1).then_inc(setup_done, 1)
            pool.wait_ge(bv_folded, 2)
            pool_norm(pool, x_in[:], 0, b_so)
            pipeline(pool, lambda it: pool_iteration(pool, it))
            ffn_gpsimd(pool)


_INS = ["x", "ctx_768", "L0_attn_Wq", "L0_attn_bq", "L0_attn_Wk", "L0_attn_bk", "L0_attn_Wv", "L0_attn_bv",
        "L0_attn_Wo", "L0_attn_bo", "L0_xattn_q_w", "L0_xattn_q_b", "L0_xattn_kv_w", "L0_xattn_kv_b",
        "L0_xattn_proj_w", "L0_xattn_proj_b", "L0_ffn_gate_w", "L0_ffn_gate_b", "L0_ffn_expert_w",
        "L0_ffn_expert_b"]


def rotation_table():
    i = np.arange(DH // 2, dtype=np.float32)
    theta = np.arange(L, dtype=np.float32)[None, :] * np.power(np.float32(10000.0), -2.0 * i / DH,
                                                               dtype=np.float32)[:, None]
    both = (np.cos(theta) + np.sin(theta)).astype(np.float32)
    return np.ascontiguousarray(np.tile(both, (2 * HT, 1)))


def kernel(**inputs):
    import concourse.bacc as bacc
    from concourse.bass_utils import run_bass_kernel_spmd

    nc = bacc.Bacc("TRN2", target_bir_lowering=False, num_devices=1)
    arrays, args = {}, []
    for name in _INS:
        a = np.ascontiguousarray(inputs[name])
        arrays[f"in_{name}"] = a
        args.append(nc.dram_tensor(f"in_{name}", a.shape, mybir.dt.from_np(a.dtype), kind="ExternalInput").ap())
    arrays["in_rotation"] = rotation_table()
    args.append(nc.dram_tensor("in_rotation", (P, L), F32, kind="ExternalInput").ap())
    args.append(nc.dram_tensor("x2_scratch", (B, L, D), F32, kind="Internal").ap())
    args.append(nc.dram_tensor("out_0", (B, L, D), F32, kind="ExternalOutput").ap())
    build_layer(nc, *args)
    return run_bass_kernel_spmd(nc, [arrays], core_ids=[0]).results[0]["out_0"]
```

```python
from contextlib import ExitStack

import concourse.bass as bass
import numpy as np
from concourse import mybir

F32 = mybir.dt.float32
F16 = mybir.dt.float16
ALU = mybir.AluOpType
ACT = mybir.ActivationFunctionType
AXIS = mybir.AxisListType

P = 128
B, L, D = 16, 100, 512
LC, DC = 722, 384
H, DH = 16, 32
E = 8
T = B * L
KD, KC = D // P, DC // P
HT = P // DH
CT = 6
CW = 121
LCP = CT * CW
HC = LC // 2
HP = LCP // 2
TT = (T + P - 1) // P
TLAST = T - (TT - 1) * P
WSCALE = 32.0
PSCALE = 1.0 / (WSCALE * WSCALE)
SOFT = PSCALE / float(np.sqrt(DH))
EPS = 1e-5
MASKED = -1e30
BANK = 512
OCOL = 304
KLOW, KHIGH, QLOW, QHIGH = range(4)

STEP_CHUNKS = [
    ["X1T", "CX0", "SQ"],
    ["CX1", "SK"],
    ["CX2", "CX3", "SV"],
    ["CX4", "CX5", "TT"],
    ["SS0", "SS1", "TP"],
    ["SS2", "SS3", "CK0"],
    ["CV0", "CK1"],
    ["SP0", "SP1", "CK2"],
    ["SP2", "SP3", "CK3"],
    ["SO0", "SO1", "CK4"],
    ["OT", "CK5", "OP"],
    ["CK6", "CK7"],
    ["X2T", "CV1", "CQ"],
    ["CV2", "CV3"],
    ["CV4"],
    ["CV5"],
]
EXP_STEPS = (5, 6)
SUM_STEPS = (6, 7)
EARLY = 11
EXTRA_CHUNKS = {
    B - 1: {0: ["FG0", "FW0"], 1: ["FW1"], 2: ["FW2", "FW3"], **{t + 3: [f"FX{t}"] for t in range(EARLY)},
            15: ["FL0"]},
    -1: {3: ["BV0", "BV1"]},
    B: {15: [f"FX{t}" for t in range(EARLY, TT)] + ["FL1"]},
}
PE_ORDER = "0SOT123"
ACT_ORDER = "0PE123"
DVE_ORDER = "M0L123"
SPLIT = ("X1T", "SV", "SP0", "SP1", "SP2", "SP3", "OT", "X2T", "TT") + tuple(
    [f"CX{c}" for c in range(6)] + ["FG0"] + [f"FW{k}" for k in range(KD)] + [f"FX{t}" for t in range(TT)]
    + [f"CK{c}" for c in range(8)] + [f"CV{c}" for c in range(6)])


class Iteration:

    def __init__(self, n, odd, cross=True, prep=True, tail=True):
        self.n, self.odd, self.cross, self.prep, self.tail = n, odd, cross, prep, tail
        self.steps = [[c for c in step if (tail if c in ("TT", "TP") else prep)] for step in STEP_CHUNKS]
        if isinstance(n, int):
            for step, chunks in EXTRA_CHUNKS.get(n, {}).items():
                self.steps[step] = self.steps[step] + chunks
        self.order = [c for step in self.steps for c in step]

    @staticmethod
    def _count(names):
        return len(names), sum(c in SPLIT for c in names)

    def _before(self, which):
        every = [c for step in STEP_CHUNKS for c in step]
        head = self._count([c for c in every if c not in ("TT", "TP")])[which]
        each = self._count(every)[which]
        prep = head
        head += self._count([c for step in EXTRA_CHUNKS[-1].values() for c in step])[which]
        if isinstance(self.n, int):
            last = ["TT", "TP"] + [c for step in EXTRA_CHUNKS[B - 1].values() for c in step]
            return 0 if self.n < 0 else head if self.n == 0 else (
                head + prep + (min(self.n, B - 1) - 1) * each + (self.n - B + 1 > 0) * self._count(last)[which])
        return head + prep + (self.n - 1) * each

    def bank(self, chunk):
        if isinstance(self.n, int) and self.n == B:
            return self.order.index(chunk) % 2
        start = self._before(0) if isinstance(self.n, int) else Iteration(2 - self.odd, self.odd)._before(0)
        return (start + self.order.index(chunk)) % 4

    def bank_free(self, chunk):
        if isinstance(self.n, int) and self.n == B:
            return max(self.done(chunk) - 2, self.all_before())
        before = self.done(chunk) - 4
        return None if isinstance(before, int) and before <= 0 else before

    def done(self, chunk):
        return self._before(0) + self.order.index(chunk) + 1

    def high_done(self, chunk):
        return self._before(1) + sum(c in SPLIT for c in self.order[:self.order.index(chunk) + 1])

    def all_before(self):
        return self._before(0)


def build_layer(nc, x, ctx, sWq, sbq, sWk, sbk, sWv, sbv, sWo, sbo, cWq, cbq, cWkv, cbkv, cWp, cbp,
                gW, gb, eW, eb, rope, x2_dram, out):
    with ExitStack() as stack:
        def sb(name, shape, dt=F32):
            return stack.enter_context(nc.sbuf_tensor(name, shape, dt))

        def sem(name):
            return stack.enter_context(nc.semaphore(name))

        w_self_all = sb("w_self_all", [P, 4, KD, 2, D], F16)
        w_self = {k: w_self_all[:, i] for i, k in enumerate("qkvo")}
        w_cross = {k: sb(f"w_cross_{k}", [P, KD, 2, D], F16) for k in "qp"}
        w_kv = sb("w_kv", [P, KC, 2, 2 * D], F16)
        ident = sb("ident", [P, P])
        mask = sb("mask", [L, L])
        rope_t = sb("rope_t", [P, L])
        b_part = sb("b_part", [P, 6, KD])
        b_rows = sb("b_rows", [6 * KD, P])
        b_value = sb("b_value", [P, 2, 2, KD], F16)
        b_so, b_cp = sb("b_so", [L, D]), sb("b_cp", [L, D])
        half = sb("half", [P, 1])
        x_in = sb("x_in", [L, D])
        x_norm = sb("x_norm", [L, D])
        s_out = x_norm
        x_mid = [sb(f"x_mid{i}", [L, D]) for i in range(2)]
        xT = sb("xT", [P, 2, KD, L], F16)
        stats = sb("stats", [P, 6])
        moments = sb("moments", [P, 2])
        shift = sb("shift", [P, 2])
        rstd = sb("rstd", [P, 1])
        tmp_q, tmp_k = sb("tmp_q", [P, KD, L]), sb("tmp_k", [P, KD, L])
        split_qk = sb("split_qk", [P, 4, KD, L], F16)
        stack_q = [sb(f"stack_q{i}", [3 * DH, H, L], F16) for i in range(2)]
        sv = sb("sv", [L, H, 2, DH], F16)
        c_raw = sb("c_raw", [CW, CT, DC])
        c_flat = c_raw[:].rearrange("p t c -> p (t c)")
        s_sc = c_flat[0:L, 0:H * L].rearrange("q (g c) -> q g c", g=4)
        s_scT = s_sc.bitcast(F16)
        s_max, s_sum, s_rinv = sb("s_max", [L, H]), sb("s_sum", [L, H]), sb("s_rinv", [L, H])
        oT = xT
        cT = sb("cT", [P, KC, 2, LCP], F16)
        split_k = sb("split_k", [P, 2, KD, LC], F16)
        cv_all = [sb(f"cv{i}", [P, CT * H * 2 * DH], F16) for i in range(2)]
        cv = [c[0:CW].rearrange("k (t h p d) -> k t h p d", t=CT, h=H, p=2) for c in cv_all]
        prob = [sb(f"prob{i}", [L, LCP]) for i in range(2)]
        probT = sb("probT", [CW, 2, CT * L], F16)
        c_max, c_bias, c_sum = (sb(n, [L, 2, H]) for n in ("c_max", "c_bias", "c_sum"))
        c_rinv = sb("c_rinv", [L, H])
        c_out = sb("c_out", [L, D])
        arena = sb("arena", [P, 2, H, LC], F16)
        stack_k = [arena[0:3 * DH, i] for i in range(2)]
        flat32 = arena[:].rearrange("p a h c -> p (a h c)").bitcast(F32)

        psum = stack.enter_context(nc.psum_tensor("psum", [P, 8, BANK], F32))
        score = psum[:, 0:2]
        pT = psum[:, 4:6]
        filler = [psum[:, b] for b in (6, 7, 2, 3)]

        const_loaded, setup_done, ident_done = sem("const_loaded"), sem("setup_done"), sem("ident_done")
        bias_ready_T, bias_done = sem("bias_ready_T"), sem("bias_done")
        raw_loaded = [sem(f"raw_loaded{i}") for i in range(5)]
        kv_loaded, p_loaded = sem("kv_loaded"), sem("p_loaded")
        wT_ready, wT_high, wT_low = sem("wT_ready"), sem("wT_high"), sem("wT_low")
        w_high, w_low = sem("w_high"), sem("w_low")
        x_loaded, ctx_loaded = sem("x_loaded"), sem("ctx_loaded")
        chunk_ready, chunk_high, chunk_out = sem("chunk_ready"), sem("chunk_high"), sem("chunk_out")
        bn_done, stats_done, ln_shift, ln_rstd, norm_done = (
            sem(n) for n in ("bn_done", "stats_done", "ln_shift", "ln_rstd", "norm_done"))
        x_biased = sem("x_biased")
        qk_rotated, qk_high, qk_split = (sem(n) for n in ("qk_rotated", "qk_high", "qk_split"))
        cq_high, cq_split = sem("cq_high"), sem("cq_split")
        s_max_done, s_shifted, s_exp, s_sum_done, s_rinv_done, s_out_done = (
            sem(n) for n in ("s_max_done", "s_shifted", "s_exp", "s_sum_done", "s_rinv_done", "s_out_done"))
        cq_stacked = [sem(f"cq_stacked{c}") for c in range(HT)]
        k_stacked = [sem(f"k_stacked{c}") for c in range(HT)]
        score_ready, max_done, bias_ready, exp_done = (
            sem(n) for n in ("score_ready", "max_done", "bias_ready", "exp_done"))
        pT_ready, pT_high, pT_low, pT_out, head_done = (
            sem(n) for n in ("pT_ready", "pT_high", "pT_low", "pT_out", "head_done"))
        c_rinv_done, c_summed, c_out_done = sem("c_rinv_done"), sem("c_summed"), sem("c_out_done")
        bv_high, bv_split = sem("bv_high"), sem("bv_split")
        x2_stored = sem("x2_stored")

        wait_over = sem("wait_over")

        def wait_alone(engine, semaphore, value):
            engine.wait_ge(semaphore, value)
            if not isinstance(value, int):
                engine.sem_inc(wait_over, 1)

        def split3(pe, out_ap, pairs):
            last = None
            for i, (a, b) in enumerate(pairs):
                for j, (pa, pb) in enumerate(((0, 0), (0, 1), (1, 0))):
                    last = pe.matmul(out_ap, a(pa), b(pb), start=(i == 0 and j == 0),
                                     stop=(i == len(pairs) - 1 and j == 2))
            return last

        raw_kv = cv_all[0].bitcast(F32)[:].rearrange("p (k f) -> p k f", k=KC)
        raw_p = cv_all[1].bitcast(F32)[:, 0:KD * D].rearrange("p (k f) -> p k f", k=KD)
        raw_q = flat32[:, 4 * KD * D:5 * KD * D].rearrange("p (k f) -> p k f", k=KD)
        arena16 = arena[:].rearrange("p a h c -> p (a h c)")
        xT3 = [(arena16[:, t * 2 * D:(t + 1) * 2 * D] if t < EARLY
                else cv_all[0][:, 2 * KD * D + (t - EARLY) * 2 * D:2 * KD * D + (t - EARLY + 1) * 2 * D])
               .rearrange("p (s k t) -> p s k t", s=2, k=KD) for t in range(TT)]
        k_flat = split_k[:].rearrange("p s k c -> p (s k c)").bitcast(F32)
        raw_e = [r.rearrange("p (o h) -> p o h", o=KD)
                 for r in (k_flat[:, 5 * TT * E:5 * TT * E + KD * D], cv_all[0].bitcast(F32)[:, 0:KD * D])]
        self32 = w_self_all[:].rearrange("p w k s f -> p (w k s f)").bitcast(F32)
        y = self32[:, 0:TT * D].rearrange("p (t d) -> p t d", t=TT)
        y_norm = [self32[:, (TT + i) * D:(TT + i + 1) * D] for i in range(2)]
        wT_e = [w_cross["q"], w_cross["p"]]
        stats3, moments3 = sb("stats3", [P, 2, 6]), sb("moments3", [P, TT, 2])
        rstd3, nmean3 = sb("rstd3", [P, TT]), sb("nmean3", [P, TT])
        g_raw, g_T, g_bias = x_in[0:E], sb("g_T", [P, 2, KD, E], F16), sb("g_bias", [P, E])
        gates, picked, first, tie, g_scaled = (
            k_flat[:, i * TT * E:(i + 1) * TT * E].rearrange("p (t e) -> p t e", e=E) for i in range(5))
        rank = sb("rank", [P, E])
        best = sb("best", [P, TT])
        g_now = sb("g_now", [P, 2, TT])
        gT_tok = c_flat[0:E, 0:TT * P].rearrange("e (t p) -> e t p", t=TT)
        e_bias = c_flat[0:E, TT * P:TT * P + D]

        y_zeroed, g_loaded = sem("y_zeroed"), sem("g_loaded")
        y_loaded = [sem(f"y_loaded{t}") for t in range(TT)]
        e_loaded = [sem(f"e_loaded{i}") for i in range(2)]
        f_bn, f_stats, f_half, f_rstd, f_norm = (sem(n) for n in ("f_bn", "f_stats", "f_half", "f_rstd", "f_norm"))
        route, g_exp = sem("route"), sem("g_exp")
        tokT_ready, tokT_out, eb_ready, eb_out = (sem(n) for n in ("tokT_ready", "tokT_out", "eb_ready", "eb_out"))
        e_T, e_high, e_low = sem("e_T"), sem("e_high"), sem("e_low")
        g_now_set, y_ready, y_done, y_stored = (sem(n) for n in ("g_now_set", "y_ready", "y_done", "y_stored"))
        rank_set = sem("rank_set")

        last_it = Iteration(B, False, cross=False, prep=False)
        ALL_CHUNKS = last_it.all_before() + len(last_it.order)
        ROUTE_STEP = 5
        ROUTED = 20

        def experts(engine, body):
            body(0, 0, 0, True)
            with engine.Fori(0, (E - 4) // 2) as i:
                body(2 * i + 1, 1, i, True)
                body(2 * i + 2, 0, i + 1, True)
            for e in range(E - 3, E):
                body(e, e % 2, e // 2, e < E - 1)

        def load_expert(sp, e, odd):
            sp.dma_start(raw_e[odd], eW[e].rearrange("(o p) h -> p o h", p=P)).then_inc(e_loaded[odd], 16)

        def load_y(sp, t):
            n = min(P, T - t * P)
            sp.wait_ge(x2_stored, 16 * ((t * P + n - 1) // L + 1))
            if t == TT - 1:
                sp.wait_ge(y_zeroed, 1)
            sp.dma_start(y[0:n, t], x2_dram.rearrange("b l d -> (b l) d")[t * P:t * P + n]).then_inc(y_loaded[t], 16)

        def ffn_sync(sp):
            sp.wait_ge(chunk_out, ALL_CHUNKS)

            def next_raw(e, odd, pair, more):
                if isinstance(e, int) and e == 0:
                    load_expert(sp, 2, 0)
                elif not isinstance(e, int) or e < E - 2:
                    wait_alone(sp, e_low, KD * e)
                    load_expert(sp, e + 2, odd)
            experts(sp, next_raw)
            for t in range(TT):
                n = min(P, T - t * P)
                sp.wait_ge(y_done, TT * (E - 1) + t + 1)
                sp.dma_start(out.rearrange("b l d -> (b l) d")[t * P:t * P + n], y[0:n, t]).then_inc(y_stored, 16)
            sp.wait_ge(y_stored, 16 * TT)

        def pe_expert_T(pe, e, odd, pair, k):
            c = KD * (e - 1) + k
            if k == 0:
                pe.wait_ge(e_loaded[odd], 16 * (pair + 1))
            if not (isinstance(c, int) and c < 2):
                pe.wait_ge(e_low, c - 1)
            for o in range(KD):
                last = pe.transpose(psum[:, 4 + k % 2, o * P:(o + 1) * P], raw_e[odd][:, o, k * P:(k + 1) * P], ident[:])
            last.then_inc(e_T, 1)

        def pe_tile(pe, e, odd, t):
            c = TT * e + t
            if not (isinstance(e, int) and c < 4):
                pe.wait_ge(y_done, c - 1 if t < 2 and not odd else c - 3)
            split3(pe, psum[:, (t + odd) % 4, 0:D],
                   [(lambda p, k=k: xT3[t][:, p, k], lambda p, k=k: wT_e[odd][:, k, p])
                    for k in range(KD)]).then_inc(y_ready, 1)

        def ffn_tensor(pe):
            def tile(e, odd, t):
                pe_tile(pe, e, odd, t)

            def bias(t):
                if t >= 2:
                    pe.wait_ge(eb_out, t - 1)
                pe.matmul(psum[:, 6 + t % 2, 0:D], gT_tok[:, t], e_bias, start=True, stop=True).then_inc(eb_ready, 1)

            def expert_0():
                for t in range(AHEAD, TT):
                    tile(0, 0, t)
                    if t % 2 == 0 and t - AHEAD < 2 * KD:
                        pe_expert_T(pe, 1, 1, 0, (t - AHEAD) // 2)
                    if t == 5:
                        pe.wait_ge(route, 2 * ROUTED)
                        for i in range(TT):
                            if i % 4 == 0 and i >= 8:
                                pe.wait_ge(tokT_out, i // 4 - 1)
                            last = pe.transpose(psum[0:E, 6 + i // 4 % 2, (i % 4) * P:(i % 4 + 1) * P], gates[:, i],
                                                ident[:])
                            if i % 4 == 3 or i == TT - 1:
                                last.then_inc(tokT_ready, 1)
                    if t == 6:
                        pe.wait_ge(tokT_out, (TT + 3) // 4)
                        pe.wait_ge(g_loaded, 32)
                    for b in bias_tiles(t):
                        bias(b)

            def expert(e, odd, pair, more):
                if isinstance(e, int) and e == 0:
                    return expert_0()
                for t in range(TT):
                    if t == 0:
                        pe.wait_ge(e_low, KD * e)
                    tile(e, odd, t)
                    if more and t % 3 == 1 and t // 3 < KD:
                        pe_expert_T(pe, e + 1, 1 - odd, pair + odd, t // 3)
            pe.wait_ge(chunk_out, ALL_CHUNKS)
            experts(pe, expert)

        AHEAD = 4

        def bias_tiles(t):
            return range(2 * (t - 6), min(2 * (t - 5), TT)) if t >= 6 else ()

        def routed_tiles(part):
            return slice(0, EARLY) if part == 0 else slice(EARLY, TT)

        def act_route(act, part):
            act.wait_ge(route, ROUTED * part + 2)
            act.activation(gates[:, routed_tiles(part)], gates[:, routed_tiles(part)], ACT.Exp).then_inc(g_exp, 1)

        def ffn_scalar(act):
            def expert_high(e, odd, k):
                act.wait_ge(e_T, KD * (e - 1) + k + 1)
                act.activation(wT_e[odd][:, k, 0], psum[:, 4 + k % 2], ACT.Copy, scale=WSCALE).then_inc(e_high, 1)

            def expert(e, odd, pair, more):
                if isinstance(e, int) and e == 0:
                    act_route(act, 1)
                for k in range(KD if more else 0):
                    expert_high(e + 1, 1 - odd, k)
                    if isinstance(e, int) and e == 0 and k == 0:
                        for i in range((TT + 3) // 4):
                            act.wait_ge(tokT_ready, i + 1)
                            n = min(4, TT - 4 * i)
                            act.activation(gT_tok[:, 4 * i:4 * i + n].rearrange("e t p -> e (t p)"),
                                           psum[0:E, 6 + i % 2, 0:n * P], ACT.Copy).then_inc(tokT_out, 1)
            experts(act, expert)

        def dve_route(dve, part):
            tiles, count = routed_tiles(part), routed_tiles(part).stop - routed_tiles(part).start
            done = [ROUTED * part]

            def step(op):
                op.then_inc(route, 1)
                done[0] += 1
                dve.wait_ge(route, done[0])

            def over(a):
                return a[:, tiles].unsqueeze(2).to_broadcast([P, count, E])
            g, pick, high, low = gates[:, tiles], picked[:, tiles], first[:, tiles], tie[:, tiles]
            most = best[:, tiles]
            step(dve.tensor_reduce(most, g, AXIS.X, ALU.max))
            step(dve.tensor_tensor(g, g, over(best), ALU.subtract))
            dve.wait_ge(g_exp, part + 1)
            step(dve.tensor_reduce(most, g, AXIS.X, ALU.add))
            step(dve.reciprocal(most, most))
            step(dve.tensor_tensor(g, g, over(best), ALU.mult))
            dve.wait_ge(rank_set, E)
            for i in range(2):
                src = g if i == 0 else low
                step(dve.tensor_reduce(most, src, AXIS.X, ALU.max))
                step(dve.tensor_tensor(high, src, over(best), ALU.is_ge))
                step(dve.tensor_tensor(high, high, rank[:].unsqueeze(1).to_broadcast([P, count, E]), ALU.mult))
                step(dve.tensor_reduce(most, high, AXIS.X, ALU.max))
                if i == 0:
                    step(dve.tensor_tensor(pick, high, over(best), ALU.is_equal))
                    step(dve.scalar_tensor_tensor(low, pick, -4.0, g, ALU.mult, ALU.add))
                else:
                    step(dve.tensor_tensor(high, high, over(best), ALU.is_equal))
                    step(dve.tensor_tensor(pick, pick, high, ALU.add))
            step(dve.tensor_tensor(g, g, pick, ALU.mult))
            step(dve.tensor_scalar(g_scaled[:, tiles], g, 1.0 / WSCALE, None, ALU.mult))
            step(dve.tensor_copy(g_now[:, 0, tiles], g_scaled[:, tiles, 0]))
            assert done[0] == ROUTED * (part + 1)

        def ffn_vector(dve):
            def expert_low(e, odd, k):
                dve.wait_ge(e_high, KD * (e - 1) + k + 1)
                dve.scalar_tensor_tensor(wT_e[odd][:, k, 1], psum[:, 4 + k % 2], WSCALE, wT_e[odd][:, k, 0],
                                         ALU.mult, ALU.subtract).then_inc(e_low, 1)
            def tile(e, odd, t):
                dve.wait_ge(y_ready, TT * e + t + 1)
                dve.scalar_tensor_tensor(y[:, t], psum[:, (t + odd) % 4, 0:D], g_now[:, odd, t:t + 1], y[:, t],
                                         ALU.mult, ALU.add).then_inc(y_done, 1)

            def expert_0():
                for t in range(TT):
                    tile(0, 0, t)
                    if t == AHEAD - 1:
                        dve.wait_ge(chunk_out, ALL_CHUNKS)
                        dve_route(dve, 1)
                    if t >= AHEAD and t % 2 == 0 and t - AHEAD < 2 * KD:
                        expert_low(1, 1, (t - AHEAD) // 2)
                    for b in bias_tiles(t):
                        dve.wait_ge(eb_ready, b + 1)
                        dve.wait_ge(y_done, b + 1)
                        dve.tensor_tensor(y[:, b], psum[:, 6 + b % 2, 0:D], y[:, b], ALU.add).then_inc(eb_out, 1)
                dve.wait_ge(eb_out, TT)

            def expert(e, odd, pair, more):
                if isinstance(e, int) and e == 0:
                    return expert_0()
                dve.wait_ge(y_done, TT * e)
                dve.tensor_copy(g_now[:, odd], g_scaled[:, :, e]).then_inc(g_now_set, 1)
                dve.wait_ge(g_now_set, e)
                for t in range(TT):
                    tile(e, odd, t)
                    if more and t % 3 == 1 and t // 3 < KD:
                        expert_low(e + 1, 1 - odd, t // 3)
            experts(dve, expert)

        def ffn_norm(pool, it, t):
            pool.wait_ge(f_stats, t + 1)
            pool.tensor_scalar(nmean3[:, t:t + 1], moments3[:, t, 0:1], -1.0, None, ALU.mult).then_inc(f_half, 1)
            pool.tensor_scalar(rstd3[:, t:t + 1], moments3[:, t, 1:2], EPS, None, ALU.add).then_inc(f_half, 1)
            pool.wait_ge(f_half, 2 * t + 2)
            pool.tensor_tensor(rstd3[:, t:t + 1], rstd3[:, t:t + 1], half[:], ALU.pow).then_inc(f_rstd, 1)
            pool.wait_ge(f_rstd, t + 1)
            if t >= 2:
                before = it if f"FX{t - 2}" in it.order else Iteration(B - 1, True, prep=False)
                pool.wait_ge(chunk_out, before.done(f"FX{t - 2}"))
            pool.tensor_scalar(y_norm[t % 2], y[:, t], nmean3[:, t:t + 1], rstd3[:, t:t + 1], ALU.add, ALU.mult)\
                .then_inc(f_norm, 1)

        def pipeline(engine, body):
            peel_from = B - 3
            body(Iteration(-1, True, cross=False, tail=False))
            body(Iteration(0, False, tail=False))
            with engine.Fori(0, (peel_from - 1) // 2) as i:
                body(Iteration(2 * i + 1, True))
                body(Iteration(2 * i + 2, False))
            for n in range(peel_from, B):
                body(Iteration(n, n % 2 == 1, prep=n < B - 1))
            body(Iteration(B, False, cross=False, prep=False))

        block = stack.enter_context(nc.Block())

        def load_x(sp, m):
            sp.dma_start(x_in[:], x[m]).then_inc(x_loaded, 16)

        def load_ctx(sp, m):
            full = CT - 1
            sp.dma_start(c_raw[:, 0:full], ctx[m, 0:full * CW].rearrange("(t p) c -> p t c", p=CW))\
              .then_inc(ctx_loaded, 16)
            sp.dma_start(c_raw[0:LC - full * CW, full], ctx[m, full * CW:LC]).then_inc(ctx_loaded, 16)

        def sync_iteration(sp, it):
            n, m = it.n, it.n + 1
            if it.tail:
                wait_alone(sp, chunk_out, it.done("TP"))
                sp.dma_start(x2_dram[n - 1], x_mid[1 if not it.odd else 0][:]).then_inc(x2_stored, 16)
                if isinstance(n, int) and n == B - 1:
                    sp.wait_ge(head_done, H * n)
                    load_expert(sp, 1, 1)
                    load_y(sp, EARLY - 1)
                elif isinstance(n, int) and n == B:
                    for t in range(EARLY, TT):
                        load_y(sp, t)
            if it.prep and not (isinstance(n, int) and n == B - 2):
                wait_alone(sp, chunk_out, it.done("SO1"))
                load_ctx(sp, n + 2)
            if it.prep:
                odd_m = not it.odd
                if not (isinstance(n, int) and n == B - 2):
                    wait_alone(sp, chunk_out, it.done("OP"))
                    load_x(sp, n + 2)
                if it.tail:
                    wait_alone(sp, score_ready, H * n)
                wait_alone(sp, chunk_out, it.done(f"CK{2 * KD - 1}"))
                for c in range(HT):
                    for r, part in enumerate((0, 0, 1)):
                        sp.dma_start(stack_k[odd_m][DH * r:DH * (r + 1), c::HT],
                                     split_k[DH * c:DH * (c + 1), part]).then_inc(k_stacked[c], 16)
                wait_alone(sp, cq_split, m + 1)
                for c in range(HT):
                    for r, slot in enumerate((QHIGH, QLOW, QHIGH)):
                        sp.dma_start(stack_q[odd_m][DH * r:DH * (r + 1), c::HT],
                                     split_qk[DH * c:DH * (c + 1), slot]).then_inc(cq_stacked[c], 16)
            if isinstance(n, int) and n == B - 2:
                for c in range(HT):
                    sp.wait_ge(k_stacked[c], 16 * 3 * B)
                sp.wait_ge(chunk_out, it.done("OP"))
                load_expert(sp, 0, 0)
                sp.dma_start(g_raw, gW).then_inc(g_loaded, 16)
                for t in range(EARLY - 1):
                    load_y(sp, t)
                sp.wait_ge(g_loaded, 16)
                sp.dma_start(e_bias, eb).then_inc(g_loaded, 16)

        @block.sync
        def _(sp):
            raw = flat32[:, 0:5 * KD * D].rearrange("p (w k f) -> p w k f", w=5, k=KD)
            load_x(sp, 0)
            sp.dma_start(raw[:, 0], sWq.rearrange("(k p) f -> p k f", p=P)).then_inc(raw_loaded[0], 16)
            sp.dma_start(rope_t[:], rope).then_inc(const_loaded, 16)
            for i, b in enumerate((sbq, sbk, cbq, cbkv[0:D], sbv, cbkv[D:2 * D])):
                sp.dma_start(b_rows[KD * i:KD * (i + 1)], b.rearrange("(m p) -> m p", p=P)).then_inc(const_loaded, 16)
            for dst, b in ((b_so, sbo), (b_cp, cbp)):
                sp.dma_start(dst[:], b.partition_broadcast(L)).then_inc(const_loaded, 16)
            sp.dma_start(g_bias[:], gb.partition_broadcast(P)).then_inc(const_loaded, 16)
            sp.dma_start(raw[:, 1], sWk.rearrange("(k p) f -> p k f", p=P)).then_inc(raw_loaded[1], 16)
            sp.wait_ge(setup_done, 2)
            load_ctx(sp, 0)
            for i, w in ((2, sWv), (3, sWo)):
                sp.dma_start(raw[:, i], w.rearrange("(k p) f -> p k f", p=P)).then_inc(raw_loaded[i], 16)
            sp.dma_start(raw_kv, cWkv.rearrange("(k p) f -> p k f", p=P)).then_inc(kv_loaded, 16)
            sp.dma_start(raw[:, 4], cWq.rearrange("(k p) f -> p k f", p=P)).then_inc(raw_loaded[4], 16)
            sp.dma_start(raw_p, cWp.rearrange("(k p) f -> p k f", p=P)).then_inc(p_loaded, 16)
            sp.wait_ge(w_low, 3)
            pipeline(sp, lambda it: sync_iteration(sp, it))
            ffn_sync(sp)

        def pe_chunk(pe, it, name):
            m = it.n + 1
            odd_m = not it.odd
            f = filler[it.bank(name)]
            if it.bank_free(name) is not None:
                pe.wait_ge(chunk_out, it.bank_free(name))
            last = None
            kind, i = name[:2], int(name[2:]) if name[2:].isdigit() else 0
            if name in ("X1T", "X2T"):
                pe.wait_ge(norm_done, 2 * m + (1 if name == "X1T" else 2))
                for k in range(KD):
                    last = pe.transpose(f[:, k * L:(k + 1) * L], x_norm[:, k * P:(k + 1) * P], ident[0:L, 0:L])
            elif kind == "BV":
                pe.wait_ge(bv_split, 1)
                pe.wait_ge(w_low, 3)
                w = (w_self["o"], w_cross["p"])[i]
                last = split3(pe, f[0:L, 0:D],
                              [(lambda p, k=k: b_value[:, i, p, k:k + 1].to_broadcast([P, L]),
                                lambda p, k=k: w[:, k, p]) for k in range(KD)])
            elif name in ("SQ", "SK", "CQ"):
                if name == "CQ" and isinstance(it.n, int) and it.n < 0:
                    pe.wait_ge(w_low, 2)
                pe.wait_ge(chunk_out, it.done("X2T" if name == "CQ" else "X1T"))
                w = w_cross["q"] if name == "CQ" else w_self[name[1].lower()]
                for o in range(KD):
                    last = split3(pe, f[:, o * L:(o + 1) * L],
                                  [(lambda p, k=k: w[:, k, p, o * P:(o + 1) * P], lambda p, k=k: xT[:, p, k])
                                   for k in range(KD)])
            elif name == "SV":
                last = split3(pe, f[0:L, 0:D], [(lambda p, k=k: xT[:, p, k], lambda p, k=k: w_self["v"][:, k, p])
                                                for k in range(KD)])
            elif kind == "SS":
                pe.wait_ge(qk_split, 2 * m + 2)
                rows = slice(DH * i, DH * (i + 1))
                for o in range(KD):
                    for c, (a, b) in enumerate(((QHIGH, KHIGH), (QHIGH, KLOW), (QLOW, KHIGH))):
                        last = pe.matmul(f[0:L, o * L:(o + 1) * L], split_qk[rows, a, o], split_qk[rows, b, o],
                                         start=c == 0, stop=c == 2)
            elif kind == "SP":
                pe.wait_ge(s_exp, 2 * m + i // 2 + 1)
                for j in range(4):
                    last = pe.transpose(f[0:L, j * L:(j + 1) * L], s_sc[:, i, j * L:(j + 1) * L], ident[0:L, 0:L])
            elif kind == "SO":
                pe.wait_ge(chunk_out, it.done("SP3"))
                for j in range(H // 2):
                    h = H // 2 * i + j
                    for p in range(2):
                        c = (p * 4 + h // 4) * L
                        last = pe.matmul(f[0:L, j * 2 * DH:(j + 1) * 2 * DH], s_scT[:, h % 4, c:c + L],
                                         sv[:, h].rearrange("k p d -> k (p d)"), start=p == 0, stop=p == 1)
            elif name in ("OT", "TT"):
                if name == "OT":
                    pe.wait_ge(s_out_done, 2 * m + 2)
                else:
                    pe.wait_ge(c_out_done, it.n)
                src = s_out if name == "OT" else c_out
                for k in range(KD):
                    last = pe.transpose(f[:, k * L:(k + 1) * L], src[:, k * P:(k + 1) * P], ident[0:L, 0:L])
            elif name in ("OP", "TP"):
                pe.wait_ge(chunk_out, it.done("OT" if name == "OP" else "TT"))
                w = w_self["o"] if name == "OP" else w_cross["p"]
                last = split3(pe, f[0:L, 0:D], [(lambda p, k=k: oT[:, p, k], lambda p, k=k: w[:, k, p])
                                                for k in range(KD)])
            elif kind == "CX":
                pe.wait_ge(ctx_loaded, 16 * 2 * (m + 1))
                k, hf = i // 2, i % 2
                for j in range(3):
                    last = pe.transpose(f[:, j * CW:(j + 1) * CW], c_raw[:, 3 * hf + j, k * P:(k + 1) * P],
                                        ident[0:CW, 0:CW])
            elif kind == "CK":
                if isinstance(it.n, int) and it.n < 0:
                    pe.wait_ge(w_low, 1)
                pe.wait_ge(chunk_out, it.done("CX5"))
                o, hf = i // 2, i % 2
                last = split3(pe, f[:, 0:HC],
                              [(lambda p, k=k: w_kv[:, k, p, o * P:(o + 1) * P],
                                lambda p, k=k: cT[:, k, p, hf * HC:(hf + 1) * HC]) for k in range(KC)])
            elif kind == "FG":
                pe.wait_ge(g_loaded, 16)
                for k in range(KD):
                    last = pe.transpose(f[:, k * E:(k + 1) * E], g_raw[:, k * P:(k + 1) * P], ident[0:E, 0:E])
            elif kind == "FW":
                pe.wait_ge(e_loaded[0], 16)
                for o in range(KD):
                    last = pe.transpose(f[:, o * P:(o + 1) * P], raw_e[0][:, o, i * P:(i + 1) * P], ident[:])
            elif kind == "FX":
                pe.wait_ge(f_norm, i + 1)
                for k in range(KD):
                    last = pe.transpose(f[:, k * P:(k + 1) * P], y_norm[i % 2][:, k * P:(k + 1) * P], ident[:])
            elif kind == "FL":
                pe.wait_ge(chunk_out, it.done(f"FX{(EARLY if i == 0 else TT) - 1}"))
                for t in (range(EARLY) if i == 0 else range(EARLY, TT)):
                    last = split3(pe, f[:, t * E:(t + 1) * E],
                                  [(lambda p, k=k: xT3[t][:, p, k], lambda p, k=k: g_T[:, p, k]) for k in range(KD)])
            elif kind == "CV":
                if isinstance(it.n, int) and it.n < 0:
                    pe.wait_ge(w_low, 1)
                pe.wait_ge(chunk_out, it.done("CX5"))
                last = split3(pe, f[0:CW, 0:D],
                              [(lambda p, k=k: cT[:, k, p, i * CW:(i + 1) * CW],
                                lambda p, k=k: w_kv[:, k, p, D:2 * D]) for k in range(KC)])
            last.then_inc(chunk_ready, 1)

        def pe_scores(pe, n, odd, h):
            g = H * n + h
            if not (isinstance(g, int) and g < 1):
                pe.wait_ge(exp_done, g)
            if h < HT:
                pe.wait_ge(k_stacked[h], 16 * 3 * (n + 1))
                pe.wait_ge(cq_stacked[h], 16 * 3 * (n + 1))
            for hf in range(2):
                last = pe.matmul(score[0:L, hf, 0:HC], stack_q[odd][:, h],
                                 stack_k[odd][:, h, hf * HC:(hf + 1) * HC], start=True, stop=True)
            last.then_inc(score_ready, 1)

        def pe_head_out(pe, n, odd, h):
            pe.wait_ge(pT_out, H * n + h + 1)
            o = OCOL + 2 * DH * (h % 2)
            for t in range(CT):
                for p in range(2):
                    last = pe.matmul(pT[0:L, h % 4 // 2, o:o + 2 * DH], probT[:, p, t * L:(t + 1) * L],
                                     cv[odd][:, t, h].rearrange("k p d -> k (p d)"),
                                     start=t + p == 0, stop=t + p == CT)
            last.then_inc(head_done, 1)

        def pe_transpose_probs(pe, n, h):
            g = H * n + h
            pe.wait_ge(exp_done, g + 1)
            if not (isinstance(g, int) and g < 1):
                pe.wait_ge(pT_out, g)
            for t in range(CT):
                last = pe.transpose(pT[0:CW, t // 3, (t % 3) * L:(t % 3 + 1) * L],
                                    prob[h % 2][:, t * CW:(t + 1) * CW], ident[0:L, 0:L])
            last.then_inc(pT_ready, 1)

        def pe_iteration(pe, it):
            n = it.n
            begun = not (isinstance(n, int) and n <= 0)
            for h in range(H):
                if isinstance(n, int) and n == B and h == H - 1:
                    pe.wait_ge(chunk_out, it.all_before())
                    for t in range(AHEAD):
                        pe_tile(pe, 0, 0, t)
                for what in PE_ORDER:
                    if what == "S":
                        if it.cross and h + 1 < H:
                            pe_scores(pe, n, it.odd, h + 1)
                        elif h + 1 == H and it.prep:
                            pe_scores(pe, n + 1, not it.odd, 0)
                    elif what == "O":
                        if h == 0 and begun:
                            pe_head_out(pe, n - 1, not it.odd, H - 1)
                        elif h > 0 and it.cross:
                            pe_head_out(pe, n, it.odd, h - 1)
                    elif what == "T":
                        if it.cross:
                            pe_transpose_probs(pe, n, h)
                    else:
                        for name in it.steps[h][int(what):][:1]:
                            pe_chunk(pe, it, name)

        @block.tensor
        def _(pe):
            pe.wait_ge(ident_done, 2)
            pe.wait_ge(const_loaded, 16 * 10)
            pe.transpose(psum[:, 7, 0:6 * KD], b_rows[:], ident[0:6 * KD, 0:6 * KD]).then_inc(bias_ready_T, 1)
            raw = flat32[:, 0:5 * KD * D].rearrange("p (w k f) -> p w k f", w=5, k=KD)
            for i in range(4 * KD):
                w, k = i // KD, i % KD
                pe.wait_ge(raw_loaded[w], 16)
                if i == 7:
                    pe.wait_ge(bias_done, 1)
                if i >= 8:
                    pe.wait_ge(wT_low, i - 7)
                for o in range(KD):
                    last = pe.transpose(psum[:, i % 8, o * P:(o + 1) * P], raw[:, w, o, k * P:(k + 1) * P], ident[:])
                last.then_inc(wT_ready, 1)
            pe.wait_ge(wT_low, 4 * KD)
            pipeline(pe, lambda it: pe_iteration(pe, it))
            ffn_tensor(pe)

        def act_chunk(act, it, name):
            if name not in SPLIT:
                return
            f = filler[it.bank(name)]
            act.wait_ge(chunk_ready, it.done(name))
            kind, i = name[:2], int(name[2:]) if name[2:].isdigit() else 0
            if name in ("X1T", "X2T", "OT", "TT"):
                dst = (xT if name[0] == "X" else oT)[:, 0].rearrange("p k l -> p (k l)")
                op = act.activation(dst, f[:, 0:KD * L], ACT.Copy)
            elif name == "SV":
                op = act.activation(sv[:, :, 0], f[0:L, 0:D].rearrange("k (h d) -> k h d", h=H), ACT.Copy)
            elif kind == "SP":
                if i % 2 == 0:
                    act.wait_ge(s_sum_done, 2 * (it.n + 1) + i // 2 + 1)
                op = act.activation(s_scT[:, i, 0:4 * L], f[0:L, 0:4 * L], ACT.Copy)
            elif kind == "CX":
                op = act.activation(cT[:, i // 2, 0, (i % 2) * HP:(i % 2 + 1) * HP], f[:, 0:HP], ACT.Copy)
            elif kind == "CK":
                if i == 0 and not (isinstance(it.n, int) and it.n < 0):
                    for c in range(HT):
                        act.wait_ge(k_stacked[c], 16 * 3 * (it.n + 1))
                op = act.activation(split_k[:, 0, i // 2, (i % 2) * HC:(i % 2 + 1) * HC], f[:, 0:HC],
                                    ACT.Identity, bias=b_part[:, 3, i // 2:i // 2 + 1])
            elif kind == "FG":
                op = act.activation(g_T[:, 0].rearrange("p k e -> p (k e)"), f[:, 0:KD * E], ACT.Copy, scale=WSCALE)
            elif kind == "FW":
                op = act.activation(wT_e[0][:, i, 0], f[:, 0:D], ACT.Copy, scale=WSCALE)
            elif kind == "FX":
                op = act.activation(xT3[i][:, 0].rearrange("p k t -> p (k t)"), f[:, 0:KD * P], ACT.Copy)
            elif kind == "CV":
                op = act.activation(cv[not it.odd][:, i, :, 0], f[0:CW, 0:D].rearrange("k (h d) -> k h d", h=H), ACT.Copy)
            op.then_inc(chunk_high, 1)

        def act_exp(act, n, odd, h):
            act.wait_ge(bias_ready, H * n + h + 1)
            act.activation(prob[h % 2][:, 0:LC].rearrange("q (a k) -> q a k", a=2), score[0:L, :, 0:HC],
                           ACT.Exp, bias=c_bias[:, int(odd), h:h + 1], scale=SOFT,
                           accum_out=c_sum[:, int(odd), h:h + 1]).then_inc(exp_done, 1)

        def act_probs_high(act, n, h):
            act.wait_ge(pT_ready, H * n + h + 1)
            act.activation(probT[:, 0].rearrange("k (a c) -> k a c", a=2), pT[0:CW, :, 0:3 * L], ACT.Copy)\
               .then_inc(pT_high, 1)

        cross_weights = ((w_kv, raw_kv, kv_loaded), (w_cross["q"], raw_q, raw_loaded[4]), (w_cross["p"], raw_p, p_loaded))

        def act_iteration(act, it):
            n = it.n
            for h in range(H):
                if isinstance(n, int) and n < 0 and 1 <= h < 4:
                    w, src, loaded = cross_weights[h - 1]
                    act.wait_ge(loaded, 16)
                    act.activation(w[:, :, 0], src, ACT.Copy, scale=WSCALE).then_inc(w_high, 1)
                if isinstance(n, int) and n == B and h == ROUTE_STEP:
                    act_route(act, 0)
                for what in ACT_ORDER:
                    if what == "E":
                        if it.cross and h + 1 < H:
                            act_exp(act, n, it.odd, h + 1)
                        elif h + 1 == H and it.prep:
                            act_exp(act, n + 1, not it.odd, 0)
                    elif what == "P":
                        if it.cross:
                            act_probs_high(act, n, h)
                    else:
                        for name in it.steps[h][int(what):][:1]:
                            act_chunk(act, it, name)
                if h in EXP_STEPS and it.prep:
                    i = EXP_STEPS.index(h)
                    act.wait_ge(s_shifted, 4 * (n + 1) + 2 * i + 2)
                    act.activation(s_sc[:, 2 * i:2 * i + 2], s_sc[:, 2 * i:2 * i + 2], ACT.Exp, scale=SOFT)\
                       .then_inc(s_exp, 1)

        @block.scalar
        def _(act):
            raw = flat32[:, 0:5 * KD * D].rearrange("p (w k f) -> p w k f", w=5, k=KD)
            for i in range(4 * KD):
                act.wait_ge(wT_ready, i + 1)
                act.activation(w_self["qkvo"[i // KD]][:, i % KD, 0], psum[:, i % 8], ACT.Copy, scale=WSCALE)\
                   .then_inc(wT_high, 1)
            act.wait_ge(bias_done, 1)
            pipeline(act, lambda it: act_iteration(act, it))
            ffn_scalar(act)

        def dve_cross_weights(dve, i):
            w, src, _ = cross_weights[i]
            dve.wait_ge(w_high, i + 1)
            dve.scalar_tensor_tensor(w[:, :, 1], src, WSCALE, w[:, :, 0], ALU.mult, ALU.subtract).then_inc(w_low, 1)

        def dve_chunk(dve, it, name):
            n, m = it.n, it.n + 1
            odd_m = not it.odd
            f = filler[it.bank(name)]
            kind, i = name[:2], int(name[2:]) if name[2:].isdigit() else 0
            if name in SPLIT:
                dve.wait_ge(chunk_high, it.high_done(name))
            else:
                dve.wait_ge(chunk_ready, it.done(name))

            def low(dst, src, high):
                return dve.tensor_tensor(dst, src, high, ALU.subtract)

            if name in ("X1T", "X2T", "OT", "TT"):
                d = xT if name[0] == "X" else oT
                op = low(d[:, 1].rearrange("p k l -> p (k l)"), f[:, 0:KD * L], d[:, 0].rearrange("p k l -> p (k l)"))
            elif name in ("SQ", "SK"):
                if not (isinstance(n, int) and n < 0):
                    dve.wait_ge(cq_split, m) if name == "SQ" else dve.wait_ge(qk_split, 2 * m)
                op = dve.tensor_tensor((tmp_q if name == "SQ" else tmp_k)[:],
                                       f[:, 0:KD * L].rearrange("p (k l) -> p k l", k=KD),
                                       b_part[:, int(name == "SK")].unsqueeze(2).to_broadcast([P, KD, L]), ALU.add)
            elif name == "CQ":
                dve.wait_ge(qk_split, 2 * m + 1)
                op = dve.tensor_tensor(tmp_q[:], f[:, 0:KD * L].rearrange("p (k l) -> p k l", k=KD),
                                       b_part[:, 2].unsqueeze(2).to_broadcast([P, KD, L]), ALU.add)
            elif name == "SV":
                op = low(sv[:, :, 1], f[0:L, 0:D].rearrange("k (h d) -> k h d", h=H), sv[:, :, 0])
            elif kind == "SS":
                op = dve.tensor_tensor(s_sc[:, i].rearrange("q (j k) -> q j k", j=4),
                                       f[0:L, 0:4 * L].rearrange("q (j k) -> q j k", j=4),
                                       mask[:].unsqueeze(1).to_broadcast([L, 4, L]), ALU.add)
            elif kind == "SP":
                op = low(s_scT[:, i, 4 * L:8 * L], f[0:L, 0:4 * L], s_scT[:, i, 0:4 * L])
            elif kind == "SO":
                parts = f[0:L].rearrange("q (h p d) -> q h p d", p=2, d=DH)
                op = dve.tensor_reduce(s_out[:, i * D // 2:(i + 1) * D // 2].rearrange("q (h d) -> q h d", h=H // 2),
                                       parts.rearrange("q h p d -> q h d p"), AXIS.X, ALU.add)
            elif kind == "BV":
                if i == 0:
                    dve.wait_ge(const_loaded, 16 * 10)
                b = (b_so, b_cp)[i]
                op = dve.scalar_tensor_tensor(b[:], f[0:L, 0:D], PSCALE, b[:], ALU.mult, ALU.add)
            elif name == "OP":
                dve.wait_ge(x_biased, 2 * m + 1)
                if not (isinstance(n, int) and n < 1):
                    dve.wait_ge(x2_stored, 16 * n)
                op = dve.scalar_tensor_tensor(x_mid[odd_m][:], f[0:L, 0:D], PSCALE, x_in[:], ALU.mult, ALU.add)
            elif name == "TP":
                buf = x_mid[not it.odd]
                dve.wait_ge(x_biased, 2 * n)
                op = dve.scalar_tensor_tensor(buf[:], f[0:L, 0:D], PSCALE, buf[:], ALU.mult, ALU.add)
            elif kind == "CX":
                c = slice((i % 2) * HP, (i % 2 + 1) * HP)
                op = low(cT[:, i // 2, 1, c], f[:, 0:HP], cT[:, i // 2, 0, c])
            elif kind == "CK":
                c = slice((i % 2) * HC, (i % 2 + 1) * HC)
                op = dve.scalar_tensor_tensor(split_k[:, 1, i // 2, c], f[:, 0:HC], b_part[:, 3, i // 2:i // 2 + 1],
                                              split_k[:, 0, i // 2, c], ALU.add, ALU.subtract)
            elif kind == "FG":
                op = dve.scalar_tensor_tensor(g_T[:, 1].rearrange("p k e -> p (k e)"), f[:, 0:KD * E], WSCALE,
                                              g_T[:, 0].rearrange("p k e -> p (k e)"), ALU.mult, ALU.subtract)
            elif kind == "FW":
                op = dve.scalar_tensor_tensor(wT_e[0][:, i, 1], f[:, 0:D], WSCALE, wT_e[0][:, i, 0],
                                              ALU.mult, ALU.subtract)
            elif kind == "FX":
                op = low(xT3[i][:, 1].rearrange("p k t -> p (k t)"), f[:, 0:KD * P],
                         xT3[i][:, 0].rearrange("p k t -> p (k t)"))
            elif kind == "FL":
                t = slice(0, EARLY) if i == 0 else slice(EARLY, TT)
                op = dve.scalar_tensor_tensor(gates[:, t], f[:, t.start * E:t.stop * E]
                                              .rearrange("p (t e) -> p t e", e=E), 1.0 / WSCALE,
                                              g_bias[:].unsqueeze(1).to_broadcast([P, t.stop - t.start, E]),
                                              ALU.mult, ALU.add)
            elif kind == "CV":
                op = low(cv[odd_m][:, i, :, 1], f[0:CW, 0:D].rearrange("k (h d) -> k h d", h=H), cv[odd_m][:, i, :, 0])
            op.then_inc(chunk_out, 1)

        def dve_max(dve, n, odd, h):
            g = H * n + h
            dve.wait_ge(score_ready, g + 1)
            if not (isinstance(g, int) and g < 2 * H):
                dve.wait_ge(exp_done, g - H)
            dve.tensor_reduce(c_max[:, int(odd), h:h + 1], score[0:L, :, 0:HC], AXIS.XY, ALU.max)\
               .then_inc(max_done, 1)
            dve.wait_ge(max_done, g + 1)
            dve.tensor_scalar(c_bias[:, int(odd), h:h + 1], c_max[:, int(odd), h:h + 1], -SOFT, None, ALU.mult)\
               .then_inc(bias_ready, 1)

        def dve_probs_low(dve, n, h):
            dve.wait_ge(pT_high, H * n + h + 1)
            return dve.tensor_tensor(probT[:, 1].rearrange("k (a c) -> k a c", a=2), pT[0:CW, :, 0:3 * L],
                                     probT[:, 0].rearrange("k (a c) -> k a c", a=2), ALU.subtract)

        def dve_inverse(dve, n, odd):
            dve.wait_ge(exp_done, H * n + H)
            if not (isinstance(n, int) and n < 1):
                dve.wait_ge(c_out_done, n)
            dve.reciprocal(c_rinv[:], c_sum[:, int(odd)]).then_inc(c_rinv_done, 1)

        def dve_heads_sum(dve, n, group):
            dve.wait_ge(head_done, H * n + 4 * group + 4)
            parts = pT[0:L, :, OCOL:OCOL + 4 * DH].rearrange("q a (b p d) -> q a b p d", p=2, d=DH)
            return dve.tensor_reduce(
                c_out[:, 4 * DH * group:4 * DH * (group + 1)].rearrange("q (a b d) -> q a b d", a=2, b=2),
                parts.rearrange("q a b p d -> q a b d p"), AXIS.X, ALU.add)

        def dve_stats(dve, src, count):
            if not (isinstance(count, int) and count < 1):
                dve.wait_ge(ln_shift, 2 * count)
            dve.bn_stats(stats[0:L], src).then_inc(bn_done, 1)
            wait_alone(dve, bn_done, count + 1)
            dve.bn_aggr(moments[0:L], stats[0:L]).then_inc(stats_done, 1)

        def ffn_stats(dve, t):
            dve.wait_ge(y_loaded[t], 16)
            if t >= 2:
                dve.wait_ge(f_stats, t - 1)
            dve.bn_stats(stats3[:, t % 2], y[:, t]).then_inc(f_bn, 1)
            dve.wait_ge(f_bn, t + 1)
            dve.bn_aggr(moments3[:, t], stats3[:, t % 2]).then_inc(f_stats, 1)

        def dve_iteration(dve, it):
            n, m = it.n, it.n + 1
            begun = not (isinstance(n, int) and n <= 0)
            for h in range(H):
                if isinstance(n, int) and n < 0 and 1 <= h < 4:
                    dve_cross_weights(dve, h - 1)
                if isinstance(n, int) and n == B - 1 and h < EARLY:
                    ffn_stats(dve, h)
                    if h == 0:
                        dve.memset(y[TLAST:P, TT - 1], 0.0).then_inc(y_zeroed, 1)
                elif isinstance(n, int) and n == B and h == H - 1:
                    for t in range(EARLY, TT):
                        ffn_stats(dve, t)
                if isinstance(n, int) and n == B and h == ROUTE_STEP:
                    dve.wait_ge(chunk_out, it.all_before())
                    dve_route(dve, 0)
                if h in SUM_STEPS and it.prep:
                    i = SUM_STEPS.index(h)
                    dve.wait_ge(s_exp, 2 * m + i + 1)
                    dve.tensor_reduce(s_sum[:, 8 * i:8 * i + 8],
                                      s_sc[:, 2 * i:2 * i + 2].rearrange("q g (j k) -> q (g j) k", j=4),
                                      AXIS.X, ALU.add).then_inc(s_sum_done, 1)
                    if i == 1:
                        dve.wait_ge(s_sum_done, 2 * m + 2)
                        dve.reciprocal(s_rinv[:].rearrange("q (o g) -> q g o", g=HT),
                                       s_sum[:].rearrange("q (g o) -> q g o", g=HT)).then_inc(s_rinv_done, 1)
                for what in DVE_ORDER:
                    if what == "M":
                        if it.cross and h + 1 < H:
                            dve_max(dve, n, it.odd, h + 1)
                        elif h + 1 == H and it.prep:
                            dve_max(dve, n + 1, not it.odd, 0)
                    elif what == "L":
                        dve_head(dve, it, h, begun)
                    else:
                        for name in it.steps[h][int(what):][:1]:
                            dve_prep(dve, it, name)
                if h == H - 2 and it.prep and not (isinstance(n, int) and n == B - 2):
                    dve.wait_ge(x_loaded, 16 * (n + 3))
                    dve_stats(dve, x_in[:], 2 * m + 2)

        def dve_head(dve, it, h, begun):
            n = it.n
            if it.cross:
                if h % 4 == 0 and (h > 0 or begun):
                    dve_probs_low(dve, n, h).then_inc(pT_low, 1)
                    dve_heads_sum(dve, n - (h == 0), (h // 4 + 3) % 4).then_inc(pT_out, 1)
                else:
                    dve_probs_low(dve, n, h).then_inc(pT_out, 1)
            elif h == 0 and begun:
                dve_heads_sum(dve, n - 1, 3).then_inc(c_summed, 1)
            if h == 0 and begun:
                dve_inverse(dve, n - 1, not it.odd)

        def dve_prep(dve, it, name):
            dve_chunk(dve, it, name)
            if name[:2] == "SS":
                i = int(name[2])
                dve.wait_ge(chunk_out, it.done(name))
                dve.tensor_reduce(s_max[:, 4 * i:4 * i + 4], s_sc[:, i].rearrange("q (j k) -> q j k", j=4),
                                  AXIS.X, ALU.max).then_inc(s_max_done, 1)
            if name == "OP":
                dve.wait_ge(chunk_out, it.done("OP"))
                dve_stats(dve, x_mid[not it.odd][:], 2 * (it.n + 1) + 1)

        @block.vector
        def _(dve):
            raw = flat32[:, 0:5 * KD * D].rearrange("p (w k f) -> p w k f", w=5, k=KD)
            dve.memset(ident[:], 0.0).then_inc(ident_done, 1)
            dve.memset(mask[:], 0.0).then_inc(setup_done, 1)
            dve.memset(c_raw[96:CW, CT - 1], 0.0).then_inc(setup_done, 1)
            for i in range(2):
                last = dve.memset(prob[i][:, LC:LCP], 0.0)
            last.then_inc(setup_done, 1)
            dve.memset(half[:], -0.5).then_inc(setup_done, 1)
            for e in range(E):
                dve.memset(rank[:, e:e + 1], float(E - e)).then_inc(rank_set, 1)
            dve.wait_ge(bias_ready_T, 1)
            dve.tensor_scalar(b_part[:].rearrange("p b k -> p (b k)"), psum[:, 7, 0:6 * KD], WSCALE, None, ALU.mult)\
               .then_inc(bias_done, 1)
            dve.wait_ge(bias_done, 1)
            dve.tensor_copy(b_value[:, :, 0], b_part[:, 4:6]).then_inc(bv_high, 1)
            dve.wait_ge(bv_high, 1)
            dve.tensor_tensor(b_value[:, :, 1], b_part[:, 4:6], b_value[:, :, 0], ALU.subtract).then_inc(bv_split, 1)
            dve.wait_ge(x_loaded, 16)
            dve_stats(dve, x_in[:], 0)
            for i in range(4 * KD):
                dve.wait_ge(wT_high, i + 1)
                w = w_self["qkvo"[i // KD]]
                dve.scalar_tensor_tensor(w[:, i % KD, 1], psum[:, i % 8], WSCALE, w[:, i % KD, 0],
                                         ALU.mult, ALU.subtract).then_inc(wT_low, 1)
            pipeline(dve, lambda it: dve_iteration(dve, it))
            ffn_vector(dve)

        def pool_norm(pool, src, count, x_bias):
            wait_alone(pool, stats_done, count + 1)
            pool.tensor_scalar(shift[0:L, 0:1], moments[0:L, 0:1], -1.0, None, ALU.mult).then_inc(ln_shift, 1)
            pool.tensor_scalar(shift[0:L, 1:2], moments[0:L, 1:2], EPS, None, ALU.add).then_inc(ln_shift, 1)
            pool.wait_ge(ln_shift, 2 * count + 2)
            pool.tensor_tensor(rstd[0:L], shift[0:L, 1:2], half[0:L], ALU.pow).then_inc(ln_rstd, 1)
            wait_alone(pool, ln_rstd, count + 1)
            pool.tensor_scalar(x_norm[:], src, shift[0:L, 0:1], rstd[0:L, 0:1], ALU.add, ALU.mult)\
                .then_inc(norm_done, 1)
            if not (isinstance(count, int) and count == 0):
                pool_bias(pool, src, count, x_bias)

        def pool_bias(pool, src, count, x_bias):
            pool.wait_ge(norm_done, count + 1)
            pool.tensor_tensor(src, src, x_bias[:], ALU.add).then_inc(x_biased, 1)

        def pool_split_q(pool, count):
            pool.tensor_copy(split_qk[:, QHIGH], tmp_q[:]).then_inc(cq_high, 1)
            pool.wait_ge(cq_high, count + 1)
            return pool.tensor_tensor(split_qk[:, QLOW], tmp_q[:], split_qk[:, QHIGH], ALU.subtract)

        def pool_iteration(pool, it):
            n, m = it.n, it.n + 1
            begun = not (isinstance(n, int) and n <= 0)
            if it.prep:
                for i, name in enumerate(("SQ", "SK")):
                    tmp, high, low = ((tmp_q, QHIGH, QLOW), (tmp_k, KHIGH, KLOW))[i]
                    rotation = rope_t[:].unsqueeze(1).to_broadcast([P, KD, L])
                    pool.wait_ge(chunk_out, it.done(name))
                    if i == 0 and not (isinstance(n, int) and n < 0):
                        for c in range(HT):
                            pool.wait_ge(cq_stacked[c], 16 * 3 * m)
                    pool.tensor_tensor(split_qk[:, high], tmp[:], rotation, ALU.mult).then_inc(qk_high, 1)
                    pool.wait_ge(qk_high, 2 * m + i + 1)
                    pool.tensor_tensor(tmp[:], tmp[:], rotation, ALU.mult).then_inc(qk_rotated, 1)
                    pool.wait_ge(qk_rotated, 2 * m + i + 1)
                    pool.tensor_tensor(split_qk[:, low], tmp[:], split_qk[:, high], ALU.subtract)\
                        .then_inc(qk_split, 1)
            if isinstance(n, int) and n < 0:
                pool.wait_ge(chunk_out, it.done("BV1"))
                pool_bias(pool, x_in[:], 0, b_so)
            if begun:
                pool.wait_ge(c_rinv_done, n)
                pool.wait_ge(pT_out, H * n + 1) if it.cross else pool.wait_ge(c_summed, 1)
                heads = c_out[:].rearrange("q (h d) -> q h d", h=H)
                pool.tensor_tensor(heads, heads, c_rinv[:].unsqueeze(2).to_broadcast([L, H, DH]), ALU.mult)\
                    .then_inc(c_out_done, 1)
            if isinstance(n, int) and n >= B - 1:
                for t in (range(EARLY) if n == B - 1 else range(EARLY, TT)):
                    ffn_norm(pool, it, t)
            if it.prep:
                for g in range(4):
                    pool.wait_ge(s_max_done, 4 * m + g + 1)
                    scores = s_sc[:, g].rearrange("q (j k) -> q j k", j=4)
                    pool.tensor_tensor(scores, scores, s_max[:, 4 * g:4 * g + 4].unsqueeze(2).to_broadcast([L, 4, L]),
                                       ALU.subtract).then_inc(s_shifted, 1)
                for i in range(2):
                    pool.wait_ge(s_rinv_done, m + 1)
                    pool.wait_ge(chunk_out, it.done(f"SO{i}"))
                    heads = s_out[:, i * D // 2:(i + 1) * D // 2].rearrange("q (h d) -> q h d", h=H // 2)
                    pool.tensor_tensor(heads, heads, s_rinv[:, i * H // 2:(i + 1) * H // 2].unsqueeze(2)
                                       .to_broadcast([L, H // 2, DH]), ALU.mult).then_inc(s_out_done, 1)
                pool_norm(pool, x_mid[not it.odd][:], 2 * m + 1, b_cp)
                wait_alone(pool, chunk_out, it.done("CQ"))
                pool_split_q(pool, m).then_inc(cq_split, 1)
                if not (isinstance(n, int) and n == B - 2):
                    pool_norm(pool, x_in[:], 2 * m + 2, b_so)

        @block.gpsimd
        def _(pool):
            pool.wait_ge(ident_done, 1)
            pool.affine_select(out=ident[:], in_=ident[:], compare_op=ALU.not_equal, fill=1.0, base=0,
                               pattern=[[-1, P]], channel_multiplier=1).then_inc(ident_done, 1)
            pool.wait_ge(setup_done, 4)
            pool.affine_select(out=mask[:], in_=mask[:], compare_op=ALU.is_ge, fill=MASKED, base=0,
                               pattern=[[-1, L]], channel_multiplier=1).then_inc(setup_done, 1)
            pool_norm(pool, x_in[:], 0, b_so)
            pipeline(pool, lambda it: pool_iteration(pool, it))


_INS = ["x", "ctx_768", "L0_attn_Wq", "L0_attn_bq", "L0_attn_Wk", "L0_attn_bk", "L0_attn_Wv", "L0_attn_bv",
        "L0_attn_Wo", "L0_attn_bo", "L0_xattn_q_w", "L0_xattn_q_b", "L0_xattn_kv_w", "L0_xattn_kv_b",
        "L0_xattn_proj_w", "L0_xattn_proj_b", "L0_ffn_gate_w", "L0_ffn_gate_b", "L0_ffn_expert_w",
        "L0_ffn_expert_b"]


def rotation_table():
    i = np.arange(DH // 2, dtype=np.float32)
    theta = np.arange(L, dtype=np.float32)[None, :] * np.power(np.float32(10000.0), -2.0 * i / DH,
                                                               dtype=np.float32)[:, None]
    both = (np.cos(theta) + np.sin(theta)).astype(np.float32)
    return np.ascontiguousarray(np.tile(both, (2 * HT, 1)))


def kernel(**inputs):
    import concourse.bacc as bacc
    from concourse.bass_utils import run_bass_kernel_spmd

    nc = bacc.Bacc("TRN2", target_bir_lowering=False, num_devices=1)
    arrays, args = {}, []
    for name in _INS:
        a = np.ascontiguousarray(inputs[name])
        arrays[f"in_{name}"] = a
        args.append(nc.dram_tensor(f"in_{name}", a.shape, mybir.dt.from_np(a.dtype), kind="ExternalInput").ap())
    arrays["in_rotation"] = rotation_table()
    args.append(nc.dram_tensor("in_rotation", (P, L), F32, kind="ExternalInput").ap())
    args.append(nc.dram_tensor("x2_scratch", (B, L, D), F32, kind="Internal").ap())
    args.append(nc.dram_tensor("out_0", (B, L, D), F32, kind="ExternalOutput").ap())
    build_layer(nc, *args)
    return run_bass_kernel_spmd(nc, [arrays], core_ids=[0]).results[0]["out_0"]
```
